# Optimizing a Trainium2 kernel written in Bass

```python
import numpy as np
import jax
import jax.numpy as jnp

def _softmax(x, axis=-1):
    return jax.nn.softmax(x, axis=axis)

def _gelu(x):
    return jax.nn.gelu(x, approximate=True)

def _silu(x):
    return jax.nn.silu(x)

def _sigmoid(x):
    return jax.nn.sigmoid(x)

def _layernorm(x, axis=-1, eps=1e-05):
    m = jnp.mean(x, axis=axis, keepdims=True)
    v = jnp.var(x, axis=axis, keepdims=True)
    return (x - m) / jnp.sqrt(v + eps)

def _scatter_add(tgt, idx, src, axis=0):
    return tgt.at[idx].add(src)

def _segment_sum(src, seg, n):
    return jax.ops.segment_sum(src, seg, n)
kernel_name = 'mk_prb_d1_jaxref_r8_febe3a'

def setup_inputs(seed: int=0):
    np.random.seed(seed)
    _w = jnp.asarray

    def _L0_attn_setup():
        import jax, jax.numpy as jnp
        import numpy as np
        D_MODEL = 256
        NUM_HEADS = 16
        D_K = D_MODEL // NUM_HEADS
        SEQ = 256
        BATCH = 2
        THETA = 10000.0

        def _rope_tables(seq_len, d_k, theta, dtype):
            pos = jnp.arange(seq_len, dtype=dtype)[:, None]
            inv = theta ** (-(jnp.arange(0, d_k, 2, dtype=dtype) / d_k))
            ang = pos * inv
            sin = jnp.repeat(jnp.sin(ang), 2, axis=1)
            cos = jnp.repeat(jnp.cos(ang), 2, axis=1)
            return (sin, cos)

        def _apply_rope(x, sin, cos):
            xp = x.reshape(x.shape[:-1] + (x.shape[-1] // 2, 2))
            swapped = jnp.stack((-xp[..., 1], xp[..., 0]), axis=-1).reshape(x.shape)
            return x * cos + swapped * sin
        key = jax.random.key(seed)
        ks = jax.random.split(key, 5)
        s = 1.0 / np.sqrt(D_MODEL)
        return {'x': jax.random.normal(ks[0], (BATCH, SEQ, D_MODEL), jnp.float32), 'wq': jax.random.normal(ks[1], (D_MODEL, D_MODEL), jnp.float32) * s, 'wk': jax.random.normal(ks[2], (D_MODEL, D_MODEL), jnp.float32) * s, 'wv': jax.random.normal(ks[3], (D_MODEL, D_MODEL), jnp.float32) * s, 'wo': jax.random.normal(ks[4], (D_MODEL, D_MODEL), jnp.float32) * s}
    _L0_attn_in = _L0_attn_setup()

    def _L0_ffn_setup():
        import jax, jax.numpy as jnp
        import numpy as np
        B, S, H = (2, 256, 256)
        E, K, I = (64, 8, 96)

        def _moe_forward(hidden_states, gate_weight, w_gate, w_up, w_down):
            b, s, h = hidden_states.shape
            x = hidden_states.reshape(-1, h)
            logits = x.astype(jnp.float32) @ gate_weight.astype(jnp.float32).T
            scores = jax.nn.softmax(logits, axis=-1)
            topk_w, topk_idx = jax.lax.top_k(scores, K)
            topk_w = topk_w / jnp.sum(topk_w, axis=-1, keepdims=True)
            flat_ids = topk_idx.reshape(-1)
            expanded = jnp.repeat(x, K, axis=0)
            order = jnp.argsort(flat_ids)
            sorted_tokens = expanded[order]
            group_sizes = jnp.zeros((E,), jnp.int32).at[flat_ids].add(1)
            g = jax.lax.ragged_dot(sorted_tokens, w_gate, group_sizes)
            u = jax.lax.ragged_dot(sorted_tokens, w_up, group_sizes)
            out = jax.lax.ragged_dot(jax.nn.silu(g) * u, w_down, group_sizes)
            inv = jnp.argsort(order)
            outs = out[inv].reshape(-1, K, h)
            y = jnp.sum(outs * topk_w[:, :, None], axis=1)
            return y.reshape(b, s, h)
        key = jax.random.key(seed)
        k0, k1, k2, k3, k4 = jax.random.split(key, 5)
        hidden_states = jax.random.normal(k0, (B, S, H), dtype=jnp.float32)
        gate_weight = jax.random.normal(k1, (E, H), dtype=jnp.float32) * 0.02
        w_gate = jax.random.normal(k2, (E, H, I), dtype=jnp.float32) * 0.02
        w_up = jax.random.normal(k3, (E, H, I), dtype=jnp.float32) * 0.02
        w_down = jax.random.normal(k4, (E, I, H), dtype=jnp.float32) * 0.02
        return {'hidden_states': hidden_states, 'gate_weight': gate_weight, 'w_gate': w_gate, 'w_up': w_up, 'w_down': w_down}
    _L0_ffn_in = _L0_ffn_setup()
    _d = {'L0_attn_x': _L0_attn_in['x'], 'L0_attn_wq': _L0_attn_in['wq'], 'L0_attn_wk': _L0_attn_in['wk'], 'L0_attn_wv': _L0_attn_in['wv'], 'L0_attn_wo': _L0_attn_in['wo'], 'L0_ffn_gate_weight': _L0_ffn_in['gate_weight'], 'L0_ffn_w_gate': _L0_ffn_in['w_gate'], 'L0_ffn_w_up': _L0_ffn_in['w_up'], 'L0_ffn_w_down': _L0_ffn_in['w_down']}
    _x0 = _d['L0_attn_x']
    _d['L0_attn_x'] = jax.random.normal(jax.random.fold_in(jax.random.key(seed), 1), (1, 1024, 256), dtype=_x0.dtype)
    del _x0
    return _d

def reference(L0_attn_x, L0_attn_wq, L0_attn_wk, L0_attn_wv, L0_attn_wo, L0_ffn_gate_weight, L0_ffn_w_gate, L0_ffn_w_up, L0_ffn_w_down):

    def _L0_attn_ref(x, wq, wk, wv, wo):
        import jax, jax.numpy as jnp
        import numpy as np
        D_MODEL = 256
        NUM_HEADS = 16
        D_K = D_MODEL // NUM_HEADS
        SEQ = 256
        BATCH = 2
        THETA = 10000.0

        def _rope_tables(seq_len, d_k, theta, dtype):
            pos = jnp.arange(seq_len, dtype=dtype)[:, None]
            inv = theta ** (-(jnp.arange(0, d_k, 2, dtype=dtype) / d_k))
            ang = pos * inv
            sin = jnp.repeat(jnp.sin(ang), 2, axis=1)
            cos = jnp.repeat(jnp.cos(ang), 2, axis=1)
            return (sin, cos)

        def _apply_rope(x, sin, cos):
            xp = x.reshape(x.shape[:-1] + (x.shape[-1] // 2, 2))
            swapped = jnp.stack((-xp[..., 1], xp[..., 0]), axis=-1).reshape(x.shape)
            return x * cos + swapped * sin
        B, S, D = x.shape
        H, dk = (NUM_HEADS, D_K)
        q = jnp.einsum('bsd,hkd->bhsk', x, wq.reshape(H, dk, D))
        k = jnp.einsum('bsd,hkd->bhsk', x, wk.reshape(H, dk, D))
        v = jnp.einsum('bsd,hkd->bhsk', x, wv.reshape(H, dk, D))
        sin, cos = _rope_tables(S, dk, THETA, x.dtype)
        q = _apply_rope(q, sin, cos)
        k = _apply_rope(k, sin, cos)
        scores = jnp.einsum('bhqk,bhsk->bhqs', q, k) / jnp.sqrt(jnp.asarray(dk, x.dtype))
        causal = jnp.triu(jnp.ones((S, S), dtype=bool), k=1)
        scores = jnp.where(causal, -jnp.inf, scores)
        attn = jax.nn.softmax(scores, axis=-1)
        out = jnp.einsum('bhqs,bhsv->bqhv', attn, v).reshape(B, S, H * dk)
        return jnp.einsum('bsf,df->bsd', out, wo)

    def _L0_ffn_ref(hidden_states, gate_weight, w_gate, w_up, w_down):
        import jax, jax.numpy as jnp
        import numpy as np
        B, S, H = (2, 256, 256)
        E, K, I = (64, 8, 96)

        def _moe_forward(hidden_states, gate_weight, w_gate, w_up, w_down):
            b, s, h = hidden_states.shape
            x = hidden_states.reshape(-1, h)
            logits = x.astype(jnp.float32) @ gate_weight.astype(jnp.float32).T
            scores = jax.nn.softmax(logits, axis=-1)
            topk_w, topk_idx = jax.lax.top_k(scores, K)
            topk_w = topk_w / jnp.sum(topk_w, axis=-1, keepdims=True)
            flat_ids = topk_idx.reshape(-1)
            expanded = jnp.repeat(x, K, axis=0)
            order = jnp.argsort(flat_ids)
            sorted_tokens = expanded[order]
            group_sizes = jnp.zeros((E,), jnp.int32).at[flat_ids].add(1)
            g = jax.lax.ragged_dot(sorted_tokens, w_gate, group_sizes)
            u = jax.lax.ragged_dot(sorted_tokens, w_up, group_sizes)
            out = jax.lax.ragged_dot(jax.nn.silu(g) * u, w_down, group_sizes)
            inv = jnp.argsort(order)
            outs = out[inv].reshape(-1, K, h)
            y = jnp.sum(outs * topk_w[:, :, None], axis=1)
            return y.reshape(b, s, h)
        return _moe_forward(hidden_states, gate_weight, w_gate, w_up, w_down)
    x = L0_attn_x
    xn = _layernorm(x, axis=-1)
    x = x + _L0_attn_ref(xn, L0_attn_wq, L0_attn_wk, L0_attn_wv, L0_attn_wo) + _L0_ffn_ref(xn, L0_ffn_gate_weight, L0_ffn_w_gate, L0_ffn_w_up, L0_ffn_w_down)
    return x

_drawn_inputs = setup_inputs


def setup_inputs(seed=0):
    import zlib

    import numpy as np

    out = dict(_drawn_inputs(seed))
    spreads = {}
    factors = {'L0_ffn_gate_weight': 8.0, 'L0_ffn_w_gate': 8.0, 'L0_ffn_w_up': 8.0, 'L0_ffn_w_down': 8.0}
    for name, (base, spread) in spreads.items():
        noise = np.random.default_rng([zlib.crc32(name.encode()), seed]).standard_normal(out[name].shape)
        drawn = base * np.exp(spread * noise) if base else spread * noise
        out[name] = jnp.asarray(drawn.astype(out[name].dtype))
    for name, factor in factors.items():
        out[name] = (out[name] * factor).astype(out[name].dtype)
    return out
```

```python
from contextlib import ExitStack

import concourse.bass as bass
from concourse import mybir

F32 = mybir.dt.float32
F32R = mybir.dt.float32r
BF16 = mybir.dt.bfloat16
I32 = mybir.dt.int32
U32 = mybir.dt.uint32
ALU = mybir.AluOpType
ACT = mybir.ActivationFunctionType
AX = mybir.AxisListType

P = 128
N = 1024
D = 256
NT = N // P
DC = D // P
H = 16
DK = D // H
HG = 4
G = H // HG
VW = 32
E = 64
K = 8
I = 96
ROW = D + 1 + 2 * K
TOK, EXP, WGT = D, D + 1, D + 1 + K
W_ROW = DC * 2 * I + D
MASKED = -1.0e30
TAKEN = -3.0e38
EPS = 1e-5
LN_FIRST = 2
PAIRS = N * K
U = 8
STEPS = (PAIRS // P + E) // U
MIN_STEPS = E // U
TILES = STEPS * U + U
NY = 4
BOUNDED = "the tables are made with first slots clamped to PAIRS and experts to E - 1"
A_BANKS = (6, 7)
STAGE_DMAS = 5
A_STEPS = ((0, 1), (2,), (3,), (4,), (5,), (6,), (7,), ())


def a_units(i):
    width = (i + 1) * P
    return [(0, width)] if width <= 512 else [(0, 512), (512, width - 512)]


def halves(kt):
    return [(max(kt * P, lo), lo + 512) for lo in (0, 512) if kt * P < lo + 512]


def wait_turn(eng, semaphore, value):
    if not isinstance(value, int) or value > 0:
        eng.wait_ge(semaphore, value)


def build(nc, x, cos, sin, w_in, w_out, w_exp, out):
    ctx = ExitStack()
    with ctx:
        def sb(name, shape, dt=F32):
            return ctx.enter_context(nc.sbuf_tensor(name, shape, dt))

        def sem(name):
            return ctx.enter_context(nc.semaphore(name))

        def dram(name, shape, dt=F32):
            return nc.dram_tensor(name, shape, dt).ap()

        WIN = 3 * D + E
        qk_parts = dram("qk_parts", [2, 2 * D, N])
        slots = dram("slots", [PAIRS + P, ROW])
        y_acc = [dram(f"y_acc{j}", [N + P, D]) for j in range(NY)]

        x_sb = sb("x_sb", [P, NT, D])
        rows = sb("rows", [P, NT, ROW])
        cos_sb = sb("cos_sb", [P, NT, DK])
        sin_sb = sb("sin_sb", [P, NT, DK])
        w_in_sb = sb("w_in_sb", [P, DC, WIN])
        w_out_sb = sb("w_out_sb", [P, DC, D])
        ident = sb("ident", [P, P])
        ones = sb("ones", [P, P])
        ident_b = sb("ident_b", [P, P], BF16)
        ones_b = sb("ones_b", [P, P], BF16)
        before_b = sb("before_b", [P, P], BF16)
        mask_kq = sb("mask_kq", [P, P], BF16)
        mask_qk = sb("mask_qk", [P, 512], BF16)
        zero = sb("zero", [P, 3 * D])
        part = sb("part", [P, 2])
        stats = sb("stats", [P, NT, 6])
        moments = sb("moments", [P, NT, 2])
        rstd = sb("rstd", [P, NT])
        var_eps = sb("var_eps", [P, NT])
        minus_half = sb("minus_half", [P, NT])
        xnT = sb("xnT", [P, DC, N])
        rope_c = sb("rope_c", [P, 2, 2 * D])
        rope_s = sb("rope_s", [P, 2, 2 * D])
        qk_rot = sb("qk_rot", [P, 2, 2 * D])
        part_hi = sb("part_hi", [P, 2, 4 * P], F32R)
        part_lo = sb("part_lo", [P, 2, 4 * P], F32R)
        v_aug = sb("v_aug", [P, NT, H, VW])
        qz = sb("qz", [P, 2, HG, N], F32R)
        kz = sb("kz", [P, 2, HG, N], F32R)
        mx = sb("mx", [P, 2, HG, NT])
        mx_low = sb("mx_low", [P, 2, HG, NT // 2])
        neg_hi = sb("neg_hi", [HG * NT, 2, P], F32R)
        neg_lo = sb("neg_lo", [HG * NT, 2, P], F32R)
        probs = sb("probs", [P, 2, HG, N])
        att_raw = sb("att_raw", [P, N])
        rec = sb("rec", [P, 4, HG])
        att = sb("att", [P, NT, D])
        attT = probs[:, 0, 0:DC, :]
        logits = sb("logits", [P, NT, E])
        top_v = sb("top_v", [P, NT, K])
        top_i = sb("top_i", [P, NT, K], U32)
        replaced = sb("replaced", [P, NT, E])
        chosen = sb("chosen", [P, NT, E], BF16)
        top_d = sb("top_d", [P, NT, K])
        top_e = sb("top_e", [P, NT, K])
        top_s = sb("top_s", [P, NT])
        top_r = sb("top_r", [P, NT])
        slot_map = replaced
        slot_f = sb("slot_f", [P, NT, K])
        slot_i = sb("slot_i", [P, NT, K], I32)
        tok_i = sb("tok_i", [P, NT], I32)
        cnt = sb("cnt", [P, E])
        end_e = sb("end_e", [P, E])
        base_e = sb("base_e", [P, E])
        n_i = sb("n_i", [P, 2, E], I32)
        n_e = sb("n_e", [P, E])
        t_end = sb("t_end", [P, E])
        t_beg = sb("t_beg", [P, E])
        shift_e = sb("shift_e", [P, E])
        is_le = sb("is_le", [P, 2, E])
        hot = sb("hot", [P, E])
        junk_e = sb("junk_e", [P, 2, E])
        col = sb("col", [P, 6])
        spread = sb("spread", [P, 3, P])
        tile_row = sb("tile_row", [1, 2 * TILES], I32)
        tile_exp = sb("tile_exp", [P, TILES])
        tile_out = sb("tile_out", [P, TILES])
        steps_f = sb("steps_f", [P, 1], I32)
        steps_i = sb("steps_i", [P, 1], I32)
        def part_of(flat, n, width, rows_=P):
            return flat[0:rows_, n * width:(n + 1) * width]

        v_flat = v_aug[:, :, :, :].rearrange("p t h c -> p (t h c)")
        probs_flat = probs[:, :, :, :].rearrange("p b h n -> p (b h n)")
        rope_s_flat = rope_s[:, :, :].rearrange("p b n -> p (b n)")
        qk_rot_flat = qk_rot[:, :, :].rearrange("p b n -> p (b n)")
        xg = [part_of(v_flat, u, ROW) for u in range(U)]
        w_all = [part_of(probs_flat, u, W_ROW) for u in range(U)]
        wgu = [w[:, 0:DC * 2 * I].rearrange("p (c i) -> p c i", c=DC) for w in w_all]
        wdn = [w[0:I, DC * 2 * I:W_ROW] for w in w_all]
        y_sb = [part_of(rope_s_flat, u, D) for u in range(NY)]
        xgT = [part_of(qk_rot_flat, u, D) for u in range(2)]
        th = [part_of(qk_rot_flat, 4 + u, P, I) for u in range(2)]
        sg = [part_of(qk_rot_flat, 6 + u, P, I) for u in range(2)]
        hidden_sb = sb("hidden_sb", [I, 2 * P])
        hh = [hidden_sb[:, u * P:(u + 1) * P] for u in range(2)]
        w_junk = [sb(f"w_junk{u}", [P, K]) for u in range(NY)]
        w_slot = [sb(f"w_slot{u}", [P, 1]) for u in range(NY)]
        dst = [sb(f"dst{u}", [P, 1], I32) for u in range(NY)]

        ps = ctx.enter_context(nc.psum_tensor("ps", [P, 8, 512], F32))

        s_x = [sem(f"x_loaded{t}") for t in range(NT)]
        s_w = sem("weights_loaded")
        s_const = sem("constants_ready")
        s_pchain = sem("pool_chain")
        s_vchain = sem("vector_chain")
        s_zero = sem("zeros_ready")
        s_clear = sem("spare_rows_set")
        s_zeroed = sem("scratch_zeroed")
        s_var = sem("variances_ready")
        s_rstd = sem("rstd_ready")
        s_ident = sem("identity_ready")
        s_xn = sem("rows_normalised")
        s_xT = sem("rows_transposed")
        s_xTe = sem("xnT_ready")
        s_proj = sem("projected")
        s_vlog = sem("v_and_logits_out")
        s_rope = sem("rope_products")
        s_rot = sem("qk_rotated")
        s_qkT = sem("qk_transposed")
        s_hi = sem("hi_ready")
        s_lo = sem("lo_ready")
        s_parts = [sem(f"parts_stored{b}") for b in range(2)]
        s_staged = [sem(f"heads_staged{b}") for b in range(2)]
        s_ap = sem("a_unit_made")
        s_ad = sem("a_unit_used")
        s_mx = sem("maxima_ready")
        s_neg = sem("negmax_ready")
        s_negd = [sem(f"negmax_placed{b}") for b in range(2)]
        s_bp = sem("scores_made")
        s_be = sem("probs_ready")
        s_pv = sem("pv_done")
        s_acc = sem("att_out")
        s_att = sem("att_normalised")
        s_aT = sem("att_transposed")
        s_aTe = sem("attT_ready")
        s_op = sem("out_projected")
        s_res = sem("residual_ready")
        s_resd = sem("residual_stored")
        s_chosen = sem("chosen_ready")
        s_d = sem("top_differences")
        s_e = sem("top_exponentials")
        s_route = sem("rows_complete")
        s_cnt = sem("counts_made")
        s_smap = sem("counts_used")
        s_sloti = sem("slot_numbers")
        s_scat = sem("rows_scattered")
        s_spread = sem("tile_columns")
        s_spread2 = sem("tile_columns_spread")
        s_table = sem("tile_tables")
        s_xg = [sem(f"tile_rows{u}") for u in range(U)]
        s_wt = [sem(f"tile_weights{u}") for u in range(U)]
        s_T = sem("tile_transposed")
        s_Te = sem("tile_xT_ready")
        s_gu = sem("tile_gate_up")
        s_th = sem("tile_tanh")
        s_sg = sem("tile_silu")
        s_h = sem("tile_hidden")
        s_dn = sem("tile_down")
        s_meta = sem("tile_destinations")
        s_y = sem("tile_result")
        s_add = [sem(f"tile_added{u}") for u in range(NY)]
        s_yl = [sem(f"sums_loaded{j}") for j in range(NY)]
        s_yp = sem("partial_sum")
        s_turn = sem("tile_may_be_added")
        s_all = sem("all_added")
        s_fin = [sem(f"final_sum{i}") for i in range(2)]
        s_out = sem("stored")

        CONSTS = 8

        a_order = []
        for g in range(-1, G + 1):
            for kt in range(NT):
                if kt == 2 and g >= 1:
                    a_order += [("post", g - 1, q) for q in range(2)]
                if g + 1 < G and g < G:
                    a_order += [("max", g + 1, i, j, u)
                                for j in range(HG) for i in A_STEPS[kt] for u in range(len(a_units(i)))]
            if g + 1 < G:
                a_order.append(("neg", g + 1))
        a_no = {key: n for n, key in enumerate(a_order)}

        def b_no(g, kt, j):
            return (g * NT + kt) * HG + j

        def sum_buf(j):
            return probs[:, j // 2, 2 * (j % 2):2 * (j % 2) + 2, :].rearrange("p a (t d) -> p (a t) d", d=D)

        block = ctx.enter_context(nc.Block())

        @block.sync
        def _(sp):
            xv = x.rearrange("(t p) d -> t p d", p=P)
            for t in range(NT):
                sp.dma_start(x_sb[:, t, :], xv[t]).then_inc(s_x[t], 16)
            sp.wait_ge(s_zero, 2)
            for b in range(2):
                for tile, lo, hi, src in ((qz, 64, P, zero), (kz, 64, 96, zero), (kz, 96, 98, ones), (kz, 98, P, zero)):
                    sp.dma_start(tile[lo:hi, b].bitcast(F32).rearrange("p h (a n) -> p (h a) n", n=P),
                                 src[lo:hi, 0:P].rearrange("p (a n) -> p a n", a=1)
                                 .to_broadcast([hi - lo, HG * NT, P])).then_inc(s_clear, 16)
            for j in range(NY):
                for r in range(0, N + P, 3 * P):
                    sp.dma_start(y_acc[j][r:r + 3 * P, :].rearrange("(p a) d -> p (a d)", a=3),
                                 zero[:, :]).then_inc(s_zeroed, 16)
            sp.dma_start(slots[PAIRS:PAIRS + P, :], zero[:, 0:ROW]).then_inc(s_zeroed, 16)
            for t in range(NT):
                for w, (tile, ready) in enumerate(((part_hi, s_hi), (part_lo, s_lo))):
                    sp.wait_ge(ready, t + 1)
                    sp.dma_start(qk_parts[w].rearrange("(b p) n -> p b n", p=P)[:, :, t * P:(t + 1) * P],
                                 tile[:, t % 2, :].bitcast(F32).rearrange("p (b n) -> p b n", n=P),
                                 ).then_inc(s_parts[t % 2], 16)

            def stage(g):
                if g >= 2:
                    sp.wait_ge(s_bp, b_no(g - 2, NT - 1, HG - 1) + 1)
                for j in range(HG):
                    f = (g * HG + j) * DK
                    q, k = qk_parts[:, f:f + DK, :], qk_parts[:, D + f:D + f + DK, :]
                    qd, kd = qz[:, g % 2, j, :].bitcast(F32), kz[:, g % 2, j, :].bitcast(F32)
                    for dst_rows, src in ((qd[0:32], q), (qd[32:64], q), (kd[0:32], k),
                                          (kd[32:48], k[1]), (kd[48:64], k[0])):
                        sp.dma_start(dst_rows, src).then_inc(s_staged[g % 2], 16)

            def place_negmax(g):
                sp.wait_ge(s_neg, g + 1)
                if g < 2:
                    sp.wait_ge(s_clear, 16 * 8)
                for r, src in ((96, neg_hi), (97, neg_lo)):
                    sp.dma_start(qz[r:r + 1, g % 2, :, :].bitcast(F32).rearrange("o h (i q) -> o (h i) q", q=P),
                                 src[:, g % 2, :].bitcast(F32)).then_inc(s_negd[g % 2], 16)

            for b in range(2):
                sp.wait_ge(s_parts[b], 16 * NT)
            stage(0)
            stage(1)
            place_negmax(0)
            for g in range(1, G):
                place_negmax(g)
                if g + 1 < G:
                    stage(g + 1)

            sp.wait_ge(s_zeroed, 16 * (3 * NY + 1))
            sp.wait_ge(s_res, NT)
            sp.dma_start(y_acc[0][0:N, :].rearrange("(t p) d -> p t d", p=P), x_sb[:, :, :]).then_inc(s_resd, 16)

            sp.wait_ge(s_table, 1)
            sp.wait_ge(s_scat, 16 * NT * K)
            sp.wait_ge(s_pv, G * NT)
            more = sp.value_load(steps_i[0:1, 0:1], min_val=MIN_STEPS - 1, max_val=STEPS - 1)

            def numbers(turn):
                _, v = nc.values_load_multi_w_load_instructions(
                    tile_row[0:1, bass.ds(turn * (2 * U), 2 * U)], engines=[mybir.EngineType.SP],
                    min_val=0, max_val=PAIRS, skip_runtime_bounds_check_because=BOUNDED)
                return [(v[2 * u], nc.s_assert_within(v[2 * u + 1], 0, E - 1,
                                                      skip_runtime_bounds_check_because=BOUNDED)) for u in range(U)]

            def load(first, expert, u, last):
                if last is not None:
                    sp.wait_ge(s_T, last + 1)
                    sp.wait_ge(s_meta, last + 1)
                sp.dma_start(xg[u], slots[bass.ds(first, P), :]).then_inc(s_xg[u], 16)
                if last is not None:
                    sp.wait_ge(s_dn, last + 1)
                sp.dma_start(w_all[u], w_exp[bass.ds(expert, 1), :, :].rearrange("a p i -> (a p) i")).then_inc(s_wt[u], 16)

            for u, (first, expert) in enumerate(numbers(0)):
                load(first, expert, u, None)
            with sp.Fori(0, STEPS) as s:
                with sp.If(s <= more):
                    for u, (first, expert) in enumerate(numbers(s + 1)):
                        load(first, expert, u, s * U + u)

            for u in range(U):
                sp.wait_ge(s_xg[u], more * 16 + 32)
                sp.wait_ge(s_wt[u], more * 16 + 32)
            for j in range(NY):
                sp.wait_ge(s_all, 1)
                sp.dma_start(sum_buf(j), y_acc[j][0:N, :].rearrange("(t p) d -> p t d", p=P)).then_inc(s_yl[j], 16)
            sp.wait_ge(s_fin[0], 1)
            sp.dma_start(out.rearrange("(t p) d -> p t d", p=P)[:, 0:NT // 2, :], sum_buf(0)[:, 0:NT // 2, :]).then_inc(s_out, 16)
            sp.wait_ge(s_fin[1], 1)
            sp.dma_start(out.rearrange("(t p) d -> p t d", p=P)[:, NT // 2:NT, :], sum_buf(0)[:, NT // 2:NT, :]).then_inc(s_out, 16)
            sp.wait_ge(s_resd, 16)
            sp.wait_ge(s_out, 32)

        @block.gpsimd
        def _(pool):
            chained = [0]

            def link(ins):
                chained[0] += 1
                ins.then_inc(s_pchain, 1)
                pool.wait_ge(s_pchain, chained[0])

            link(pool.memset(ident[:, :], 0.0))
            pool.affine_select(out=ident[:, :], in_=ident[:, :], compare_op=ALU.not_equal, fill=1.0, base=0,
                               pattern=[[-1, P]], channel_multiplier=1).then_inc(s_ident, 1)
            pool.memset(zero[:, :], 0.0).then_inc(s_zero, 1)
            pool.memset(ones[:, :], 1.0).then_inc(s_zero, 1)
            link(pool.memset(minus_half[:, :], -0.5))
            for n, (lo, hi) in enumerate(((0, LN_FIRST), (LN_FIRST, NT))):
                pool.wait_ge(s_var, hi)
                pool.tensor_tensor(rstd[:, lo:hi], var_eps[:, lo:hi], minus_half[:, lo:hi], ALU.pow).then_inc(s_rstd, 1)
            link(pool.memset(ident_b[:, :], 0.0))
            pool.affine_select(out=ident_b[:, :], in_=ident_b[:, :], compare_op=ALU.not_equal, fill=1.0, base=0,
                               pattern=[[-1, P]], channel_multiplier=1).then_inc(s_const, 1)
            pool.memset(ones_b[:, :], 1.0).then_inc(s_const, 1)
            link(pool.memset(before_b[:, :], 1.0))
            pool.affine_select(out=before_b[:, :], in_=before_b[:, :], compare_op=ALU.is_gt, fill=0.0, base=0,
                               pattern=[[1, P]], channel_multiplier=-1).then_inc(s_const, 1)
            link(pool.memset(mask_kq[:, :], 0.0))
            pool.affine_select(out=mask_kq[:, :], in_=mask_kq[:, :], compare_op=ALU.is_ge, fill=MASKED, base=0,
                               pattern=[[1, P]], channel_multiplier=-1).then_inc(s_const, 1)
            link(pool.memset(mask_qk[:, :], 0.0))
            pool.affine_select(out=mask_qk[:, :], in_=mask_qk[:, :], compare_op=ALU.is_ge, fill=MASKED, base=512 - P,
                               pattern=[[-1, 512]], channel_multiplier=1).then_inc(s_const, 1)
            pool.iota(tok_i[:, :], [[P, NT]], base=0, channel_multiplier=1).then_inc(s_const, 1)
            pool.iota(part[:, :], [[N, 2]], base=0, channel_multiplier=1,
                      allow_small_or_imprecise_dtypes=True).then_inc(s_const, 1)
            link(pool.memset(v_aug[:, :, :, DK:VW], 0.0))
            pool.memset(v_aug[:, :, :, DK:DK + 1], 1.0).then_inc(s_const, 1)

            for t in range(NT):
                pool.wait_ge(s_rope, 3 * (t + 1))
                if t >= 2:
                    pool.wait_ge(s_qkT, t - 1)
                pool.tensor_tensor(qk_rot[:, t % 2, :], rope_c[:, t % 2, :], rope_s[:, t % 2, :],
                                   ALU.add).then_inc(s_rot, 1)

            pool.wait_ge(s_route, 1)
            pool.wait_ge(s_sloti, 1)
            for t in range(NT):
                for k in range(K):
                    pool.indirect_dma_start(slots[:, :], bass.IndirectOffsetOnAxis(ap=slot_i[:, t, k:k + 1], axis=0),
                                            rows[:, t, :], None).then_inc(s_scat, 16)

            pool.wait_ge(s_resd, 16)
            pool.wait_ge(s_zeroed, 16 * (3 * NY + 1))

            def add(n, u, before):
                pool.wait_ge(s_y, n + 1)
                wait_turn(pool, s_add[u], 16 * before)
                pool.sem_inc(s_turn, 1)
                pool.indirect_dma_start(y_acc[u][:, :], bass.IndirectOffsetOnAxis(ap=dst[u][:, 0:1], axis=0),
                                        y_sb[u], None, compute_op=ALU.add).then_inc(s_add[u], 16)

            more = pool.value_load(steps_i[0:1, 0:1], min_val=MIN_STEPS - 1, max_val=STEPS - 1)

            def step(s):
                for u in range(1, U + 1):
                    add(s * U + u, u % NY, s * (U // NY) + u // NY)

            add(0, 0, 0)
            step(0)
            with pool.Fori(1, STEPS) as s:
                with pool.If(s <= more):
                    step(s)
            pool.wait_ge(s_add[0], more * (16 * U // NY) + 16 * U // NY + 16)
            for u in range(1, NY):
                pool.wait_ge(s_add[u], more * (16 * U // NY) + 16 * U // NY)
            pool.sem_inc(s_all, 1)
            for j in range(NY):
                pool.wait_ge(s_yl[j], 16)
            h = slice(NT // 2, NT)
            link(pool.tensor_tensor(sum_buf(2)[:, h], sum_buf(2)[:, h], sum_buf(3)[:, h], ALU.add))
            pool.drain().then_inc(s_yp, 1)

        @block.scalar
        def _(act):
            act.dma_start(cos_sb[:, :, :], cos).then_inc(s_w, 16)
            act.dma_start(sin_sb[:, :, :], sin).then_inc(s_w, 16)
            act.dma_start(w_in_sb[:, :, :], w_in.rearrange("(c p) n -> p c n", p=P)).then_inc(s_w, 16)
            act.dma_start(w_out_sb[:, :, :], w_out.rearrange("(c p) n -> p c n", p=P)).then_inc(s_w, 16)

            def xT_out(t):
                act.wait_ge(s_xT, t + 1)
                act.activation(xnT[:, :, t * P:(t + 1) * P],
                               ps[:, t % 2, 0:DC * P].rearrange("p (c n) -> p c n", n=P), ACT.Copy).then_inc(s_xTe, 1)

            def v_out(t):
                act.wait_ge(s_proj, t + 1)
                act.activation(v_aug[:, t, :, 0:DK], ps[:, 4 + t % 2, 0:D].rearrange("p (h c) -> p h c", c=DK), ACT.Copy)
                act.activation(logits[:, t, :], ps[:, 4 + t % 2, D:D + E], ACT.Copy).then_inc(s_vlog, 1)

            def hi_out(t):
                act.wait_ge(s_qkT, t + 1)
                if t >= 2:
                    act.wait_ge(s_parts[t % 2], 32 * (t // 2))
                act.activation(part_hi[:, t % 2, :], ps[:, 6 + t % 2, :], ACT.Copy).then_inc(s_hi, 1)

            xT_out(0)
            for t in range(NT):
                if t + 1 < NT:
                    xT_out(t + 1)
                v_out(t)
                if t >= 1:
                    hi_out(t - 1)
            hi_out(NT - 1)

            def exps(g, kt, j):
                n = b_no(g, kt, j)
                act.wait_ge(s_bp, n + 1)
                if kt * HG + j >= 2 * HG or g > 0:
                    act.wait_ge(s_pv, g * NT + kt - 1)
                act.activation(probs[:, kt % 2, j, kt * P:N],
                               ps[:, 2 * (n % 2):2 * (n % 2) + 2, :].rearrange("p a b -> p (a b)")[:, kt * P:N],
                               ACT.Exp, scale=DK ** -0.5).then_inc(s_be, 1)

            def att_out(g):
                act.wait_ge(s_pv, (g + 1) * NT)
                if g >= 1:
                    act.wait_ge(s_ap, a_no[("post", g - 1, 1)] + 1)
                act.activation(att_raw[:, :], ps[:, 4:6, :].rearrange("p a b -> p (a b)"), ACT.Copy).then_inc(s_acc, 1)

            for g in range(G):
                for kt in range(NT):
                    for j in range(HG):
                        exps(g, kt, j)
                    if g == 0 and kt == 0:
                        act.wait_ge(s_d, 1)
                        act.activation(top_e[:, :, :], top_d[:, :, :], ACT.Exp).then_inc(s_e, 1)
                    if g > 0 and kt == 0:
                        att_out(g - 1)
            att_out(G - 1)
            for t in range(NT):
                act.wait_ge(s_aT, t + 1)
                act.activation(attT[:, :, t * P:(t + 1) * P],
                               ps[:, t % 2, 0:DC * P].rearrange("p (c n) -> p c n", n=P), ACT.Copy).then_inc(s_aTe, 1)

            act.wait_ge(s_table, 1)
            more = act.value_load(steps_i[0:1, 0:1], min_val=MIN_STEPS - 1, max_val=STEPS - 1)

            def tanh(n, b):
                act.wait_ge(s_gu, n + 1)
                wait_turn(act, s_h, n - 1)
                act.activation(th[b], ps[0:I, 2 + b, 0:P], ACT.Tanh, scale=0.5).then_inc(s_th, 1)

            def result(n, u, b, added):
                act.wait_ge(s_dn, n + 1)
                act.wait_ge(s_meta, n + 1)
                wait_turn(act, s_add[u], 16 * added)
                act.activation(y_sb[u], ps[:, 4 + b, 0:D], ACT.Copy, scale=w_slot[u][:, 0:1]).then_inc(s_y, 1)

            def step(s):
                for u in range(1, U + 1):
                    n = s * U + u
                    tanh(n, u % 2)
                    result(n - 1, (u - 1) % NY, (u - 1) % 2, s * (U // NY) + (u - 1) // NY)

            tanh(0, 0)
            step(0)
            with act.Fori(1, STEPS) as s:
                with act.If(s <= more):
                    step(s)
            result(more * U + U, 0, 0, more * (U // NY) + U // NY)

        @block.tensor
        def _(pe):
            def x_transpose(t):
                pe.wait_ge(s_xn, t + 1)
                if t >= 2:
                    pe.wait_ge(s_xTe, t - 1)
                for c in range(DC):
                    last = pe.transpose(ps[:, t % 2, c * P:(c + 1) * P], rows[:, t, c * P:(c + 1) * P], ident[:, :])
                last.then_inc(s_xT, 1)

            def project(t):
                pe.wait_ge(s_xTe, t + 1)
                if t >= 2:
                    pe.wait_ge(s_rope, 3 * (t - 1))
                    pe.wait_ge(s_vlog, t - 1)
                for bank, lo, hi in ((4, 2 * D, WIN), (2, 0, 2 * D)):
                    for c in range(DC):
                        last = pe.matmul(ps[:, bank + t % 2, 0:hi - lo], xnT[:, c, t * P:(t + 1) * P],
                                         w_in_sb[:, c, lo:hi], start=(c == 0), stop=(c == DC - 1))
                last.then_inc(s_proj, 1)

            def qk_transpose(t):
                pe.wait_ge(s_rot, t + 1)
                if t >= 2:
                    pe.wait_ge(s_lo, t - 1)
                for b in range(4):
                    last = pe.transpose(ps[:, 6 + t % 2, b * P:(b + 1) * P], qk_rot[:, t % 2, b * P:(b + 1) * P],
                                        ident[:, :])
                last.then_inc(s_qkT, 1)

            pe.wait_ge(s_ident, 1)
            x_transpose(0)
            pe.wait_ge(s_w, 64)
            for t in range(NT):
                if t + 1 < NT:
                    x_transpose(t + 1)
                project(t)
                if t >= 1:
                    qk_transpose(t - 1)
            qk_transpose(NT - 1)

            pe.wait_ge(s_const, CONSTS)
            pe.wait_ge(s_chosen, 1)
            pe.wait_ge(s_vlog, NT)
            pe.wait_ge(s_rope, 3 * NT)
            for t in range(NT):
                pe.matmul(ps[:, 4, 0:E], ones_b[:, :], chosen[:, t, :], start=(t == 0), stop=(t == NT - 1))
            for t in range(NT):
                for s in range(t + 1):
                    last = pe.matmul(ps[:, 5, t * E:(t + 1) * E], before_b[:, :] if s == t else ones_b[:, :],
                                     chosen[:, s, :], start=(s == 0), stop=(s == t))
            last.then_inc(s_cnt, 1)

            def a_free(key):
                n = a_no[key]
                if n >= 2:
                    pe.wait_ge(s_ad, n - 1)
                elif n == 0:
                    pe.wait_ge(s_lo, NT)
                return ps[:, A_BANKS[n % 2], :]

            def max_scores(g, i, j):
                for u, (lo, width) in enumerate(a_units(i)):
                    bank = a_free(("max", g, i, j, u))
                    pe.matmul(bank[:, 0:width], qz[0:96, g % 2, j, i * P:(i + 1) * P],
                              kz[0:96, g % 2, j, lo:lo + width], start=True, stop=True).then_inc(s_ap, 1)

            def neg_transpose(g):
                key = ("neg", g)
                bank = a_free(key)
                pe.wait_ge(s_mx, g + 1)
                pe.transpose(bank[0:HG * NT, 0:P], mx[:, g % 2, :, :].rearrange("p h i -> p (h i)"),
                             ident[:, :]).then_inc(s_ap, 1)

            def scores(g, kt, j):
                n = b_no(g, kt, j)
                if n >= 2:
                    pe.wait_ge(s_be, n - 1)
                else:
                    pe.wait_ge(s_rope, 3 * NT)
                two = ps[:, 2 * (n % 2):2 * (n % 2) + 2, :].rearrange("p a b -> p (a b)")
                for lo, hi in halves(kt):
                    diagonal = lo == kt * P
                    last = pe.matmul(two[:, lo:hi], kz[:, g % 2, j, kt * P:(kt + 1) * P], qz[:, g % 2, j, lo:hi],
                                     start=True, stop=True, skip_group_check=True)
                    if diagonal:
                        last = pe.matmul(two[:, lo:lo + P], ident_b[:, :], mask_kq[:, :], start=False, stop=True,
                                         skip_group_check=True)
                last.then_inc(s_bp, 1)

            def pv(g, kt):
                pe.wait_ge(s_be, b_no(g, kt, HG - 1) + 1)
                if kt == 0 and g >= 1:
                    pe.wait_ge(s_acc, g)
                for lo, hi in halves(kt):
                    for j in range(HG):
                        last = pe.matmul(ps[VW * j:VW * (j + 1), 4 + lo // 512, lo % 512:(hi - 1) % 512 + 1],
                                         v_aug[:, kt, g * HG + j, :], probs[:, kt % 2, j, lo:hi],
                                         start=(kt == 0), stop=True,
                                         skip_group_check=True)
                last.then_inc(s_pv, 1)

            def post(g, q):
                bank = a_free(("post", g, q))
                pe.wait_ge(s_acc, g + 1)
                for t in range(4):
                    last = pe.transpose(bank[:, t * P:(t + 1) * P], att_raw[:, (4 * q + t) * P:(4 * q + t + 1) * P],
                                        ident[:, :])
                last.then_inc(s_ap, 1)

            for g in range(-1, G + 1):
                for kt in range(NT):
                    if kt == 0 and 0 <= g < G:
                        pe.wait_ge(s_negd[g % 2], 32 * (g // 2 + 1))
                    if kt == 0 and g == -1:
                        pe.wait_ge(s_clear, 16 * 8)
                    if kt == 0 and g + 1 < G:
                        pe.wait_ge(s_staged[(g + 1) % 2], 16 * STAGE_DMAS * HG * ((g + 1) // 2 + 1))
                    if kt == 0 and g == 0:
                        pe.wait_ge(s_smap, 1)
                    if kt == 2 and g >= 1:
                        post(g - 1, 0)
                        post(g - 1, 1)
                    for j in range(HG):
                        if 0 <= g < G:
                            scores(g, kt, j)
                        if g + 1 < G:
                            for i in A_STEPS[kt]:
                                max_scores(g + 1, i, j)
                    if 0 <= g < G and kt >= 1:
                        pv(g, kt - 1)
                    if kt == 0 and g >= 1:
                        pv(g - 1, NT - 1)
                if g + 1 < G:
                    neg_transpose(g + 1)

            pe.wait_ge(s_spread, 1)
            pe.matmul(ps[:, 4, 0:3 * P], ones[:, :], spread[:, :, :].rearrange("p a b -> p (a b)"),
                      start=True, stop=True).then_inc(s_spread2, 1)

            pe.wait_ge(s_att, 2 * G)
            for t in range(NT + 1):
                if t < NT:
                    if t >= 2:
                        pe.wait_ge(s_aTe, t - 1)
                    for c in range(DC):
                        last = pe.transpose(ps[:, t % 2, c * P:(c + 1) * P], att[:, t, c * P:(c + 1) * P], ident[:, :])
                    last.then_inc(s_aT, 1)
                if t >= 1:
                    o = t - 1
                    pe.wait_ge(s_aTe, o + 1)
                    if o >= 2:
                        pe.wait_ge(s_res, o - 1)
                    for c in range(DC):
                        last = pe.matmul(ps[:, 2 + o % 2, 0:D], attT[:, c, o * P:(o + 1) * P], w_out_sb[:, c, :],
                                         start=(c == 0), stop=(c == DC - 1))
                    last.then_inc(s_op, 1)

            pe.wait_ge(s_aTe, NT)
            pe.wait_ge(s_res, NT)
            pe.wait_ge(s_table, 1)
            more = pe.value_load(steps_i[0:1, 0:1], min_val=MIN_STEPS - 1, max_val=STEPS - 1)

            def transpose_rows(n, u, b, turn):
                pe.wait_ge(s_xg[u], 16 * turn + 16)
                wait_turn(pe, s_Te, n - 1)
                for c in range(DC):
                    last = pe.transpose(ps[:, b, c * P:(c + 1) * P], xg[u][:, c * P:(c + 1) * P], ident[:, :])
                last.then_inc(s_T, 1)

            def gate_up(n, u, b, turn):
                pe.wait_ge(s_Te, n + 1)
                pe.wait_ge(s_wt[u], 16 * turn + 16)
                wait_turn(pe, s_h, n - 1)
                for w in range(2):
                    for c in range(DC):
                        last = pe.matmul(ps[0:I, 2 + b, w * P:(w + 1) * P], wgu[u][:, c, w * I:(w + 1) * I],
                                         xgT[b][:, c * P:(c + 1) * P], start=(c == 0), stop=(c == DC - 1))
                last.then_inc(s_gu, 1)

            def down(n, u, b):
                pe.wait_ge(s_h, n + 1)
                pe.matmul(ps[:, 4 + b, 0:D], hh[b], wdn[u], start=True, stop=True).then_inc(s_dn, 1)

            def step(s):
                for u in range(1, U + 1):
                    n = s * U + u
                    gate_up(n, u % U, u % 2, s + u // U)
                    transpose_rows(n + 2, (u + 2) % U, u % 2, s + (u + 2) // U)
                    down(n - 1, (u - 1) % U, (u - 1) % 2)
                    wait_turn(pe, s_y, n - 1)

            transpose_rows(0, 0, 0, 0)
            transpose_rows(1, 1, 1, 0)
            gate_up(0, 0, 0, 0)
            transpose_rows(2, 2, 0, 0)
            step(0)
            with pe.Fori(1, STEPS) as s:
                with pe.If(s <= more):
                    step(s)
            down(more * U + U, 0, 0)

        @block.vector
        def _(dve):
            chained = [0]

            def link(ins):
                chained[0] += 1
                ins.then_inc(s_vchain, 1)
                dve.wait_ge(s_vchain, chained[0])

            def measure(t):
                dve.wait_ge(s_x[t], 16)
                link(dve.bn_stats(stats[:, t, :], x_sb[:, t, :]))
                link(dve.bn_aggr(moments[:, t, :], stats[:, t, :]))
                dve.tensor_scalar(var_eps[:, t:t + 1], moments[:, t, 1:2], EPS, None, ALU.add).then_inc(s_var, 1)

            def normalise(t):
                dve.wait_ge(s_rstd, 1 if t < LN_FIRST else 2)
                dve.tensor_scalar(rows[:, t, 0:D], x_sb[:, t, :], moments[:, t, 0:1], rstd[:, t:t + 1],
                                  ALU.subtract, ALU.mult).then_inc(s_xn, 1)

            def rotate(t):
                dve.wait_ge(s_proj, t + 1)
                if t >= 2:
                    dve.wait_ge(s_rot, t - 1)
                heads = 2 * D // DK
                qk = ps[:, 2 + t % 2, :].rearrange("p (h c) -> p h c", c=DK)

                def table(tab):
                    return tab[:, t, :].rearrange("p (a c) -> p a c", a=1).to_broadcast([P, heads, DK])

                dve.tensor_tensor(rope_c[:, t % 2, :].rearrange("p (h c) -> p h c", c=DK), qk, table(cos_sb),
                                  ALU.mult).then_inc(s_rope, 1)
                for odd in range(2):
                    dve.tensor_tensor(rope_s[:, t % 2, :].rearrange("p (h c) -> p h c", c=DK)[:, :, odd::2],
                                      qk[:, :, 1 - odd::2], table(sin_sb)[:, :, odd::2], ALU.mult).then_inc(s_rope, 1)

            def lo_out(t):
                dve.wait_ge(s_hi, t + 1)
                if t >= 2:
                    dve.wait_ge(s_parts[t % 2], 32 * (t // 2))
                dve.tensor_tensor(part_lo[:, t % 2, :], ps[:, 6 + t % 2, :], part_hi[:, t % 2, :].bitcast(F32),
                                  ALU.subtract).then_inc(s_lo, 1)

            for t in range(NT):
                measure(t)
                if t == LN_FIRST:
                    for first in range(LN_FIRST):
                        normalise(first)
            normalise(LN_FIRST)
            dve.wait_ge(s_w, 64)
            for t in range(NT):
                rotate(t)
                if t + LN_FIRST + 1 < NT:
                    normalise(t + LN_FIRST + 1)
                if t >= 1:
                    lo_out(t - 1)
            lo_out(NT - 1)

            dve.wait_ge(s_vlog, NT)
            dve.wait_ge(s_const, CONSTS)
            for t in range(NT):
                last = dve.max(top_v[:, t, :], logits[:, t, :])
            link(last)
            for t in range(NT):
                dve.match_replace(replaced[:, t, :], top_v[:, t, :], logits[:, t, :], TAKEN)
                last = dve.max_index(top_i[:, t, :], top_v[:, t, :], logits[:, t, :])
            link(last)
            dve.tensor_scalar(chosen[:, :, :], replaced[:, :, :], TAKEN, None, ALU.is_equal).then_inc(s_chosen, 1)
            dve.tensor_tensor(top_d[:, :, :], top_v[:, :, :], top_v[:, :, 0:1].to_broadcast([P, NT, K]),
                              ALU.subtract).then_inc(s_d, 1)
            dve.tensor_copy(rows[:, :, EXP:EXP + K], top_i[:, :, :])
            link(dve.tensor_copy(rows[:, :, TOK:TOK + 1], tok_i[:, :].rearrange("p (t a) -> p t a", a=1)))

            def count_and_map():
                dve.wait_ge(s_cnt, 1)
                link(dve.tensor_copy(cnt[:, :], ps[:, 4, 0:E]))
                link(dve.tensor_tensor_scan(end_e[:, :], ones[:, 0:E], cnt[:, :], 0.0, ALU.mult, ALU.add))
                link(dve.tensor_tensor(base_e[:, :], end_e[:, :], cnt[:, :], ALU.subtract))
                link(dve.scalar_tensor_tensor(slot_map[:, :, :], ps[:, 5, :].rearrange("p (t e) -> p t e", e=E), 1.0,
                                              base_e[:, :].rearrange("p (a e) -> p a e", a=1)
                                              .to_broadcast([P, NT, E]), ALU.add, ALU.add))
                dve.sem_inc(s_smap, 1)
                link(dve.tensor_tensor(slot_map[:, :, :], slot_map[:, :, :], chosen[:, :, :], ALU.mult))
                for t in range(NT):
                    last = dve.max(slot_f[:, t, :], slot_map[:, t, :])
                link(last)
                dve.tensor_scalar(slot_i[:, :, :], slot_f[:, :, :], -1.0, None, ALU.add).then_inc(s_sloti, 1)

            def weights():
                dve.wait_ge(s_e, 1)
                link(dve.tensor_reduce(top_s[:, :], top_e[:, :, :], AX.X, ALU.add))
                link(dve.reciprocal(top_r[:, :], top_s[:, :]))
                dve.scalar_tensor_tensor(rows[:, :, WGT:WGT + K], top_e[:, :, :], 0.5,
                                         top_r[:, :].rearrange("p (t a) -> p t a", a=1).to_broadcast([P, NT, K]),
                                         ALU.mult, ALU.mult).then_inc(s_route, 1)

            def tile_columns():
                link(dve.tensor_scalar(n_i[:, 0, :], cnt[:, :], float(P - 1), None, ALU.add))
                link(dve.tensor_scalar(n_i[:, 1, :], n_i[:, 0, :], P.bit_length() - 1, None, ALU.arith_shift_right))
                link(dve.tensor_scalar(n_e[:, :], n_i[:, 1, :], 1.0, None, ALU.max))
                link(dve.tensor_tensor_scan(t_end[:, :], ones[:, 0:E], n_e[:, :], 0.0, ALU.mult, ALU.add))
                dve.tensor_scalar(steps_f[:, :], t_end[:, E - 1:E], -2.0, None, ALU.add)
                link(dve.tensor_tensor(t_beg[:, :], t_end[:, :], n_e[:, :], ALU.subtract))
                dve.tensor_scalar(steps_i[:, :], steps_f[:, :], U.bit_length() - 1, None, ALU.arith_shift_right)
                dve.scalar_tensor_tensor(shift_e[:, :], t_beg[:, :], -float(P), base_e[:, :], ALU.mult, ALU.add)
                dve.tensor_scalar(is_le[:, 0, :], t_beg[:, :], part[:, 0:1], None, ALU.is_le)
                link(dve.tensor_scalar(is_le[:, 1, :], t_end[:, :], part[:, 0:1], None, ALU.is_le))
                dve.tensor_reduce(col[:, 0:1], is_le[:, 1, :], AX.X, ALU.add)
                link(dve.tensor_tensor(hot[:, :], is_le[:, 0, :], is_le[:, 1, :], ALU.subtract))
                dve.tensor_tensor_reduce(junk_e[:, 0, :], hot[:, :], shift_e[:, :], 1.0, 0.0, ALU.mult, ALU.add,
                                         col[:, 1:2])
                link(dve.tensor_tensor_reduce(junk_e[:, 1, :], hot[:, :], end_e[:, :], 1.0, 0.0, ALU.mult, ALU.add,
                                              col[:, 2:3]))
                dve.tensor_scalar(col[:, 3:4], col[:, 0:1], float(E - 1), None, ALU.min)
                link(dve.scalar_tensor_tensor(col[:, 4:5], part[:, 0:1], float(P), col[:, 1:2], ALU.mult, ALU.add))
                link(dve.tensor_scalar(col[:, 4:5], col[:, 4:5], float(PAIRS), None, ALU.min))
                link(dve.tensor_tensor(col[:, 5:6], col[:, 2:3], col[:, 4:5], ALU.subtract))
                for a, c in enumerate((4, 3, 5)):
                    last = dve.tensor_scalar(spread[:, a, :], ident[:, :], col[:, c:c + 1], None, ALU.mult)
                last.then_inc(s_spread, 1)

            def tables():
                link(dve.memset(tile_row[:, 0::2], PAIRS))
                dve.memset(tile_row[:, 1::2], 0)
                dve.memset(tile_exp[:, :], 0.0)
                link(dve.tensor_copy(tile_out[:, :], part[:, 1:2].to_broadcast([P, TILES])))
                dve.wait_ge(s_spread2, 1)
                dve.tensor_copy(tile_row[0:1, 0:2 * P:2], ps[0:1, 4, 0:P])
                dve.tensor_copy(tile_row[0:1, 1:2 * P:2], ps[0:1, 4, P:2 * P])
                dve.tensor_copy(tile_exp[:, 0:P], ps[:, 4, P:2 * P])
                dve.tensor_scalar(tile_out[:, 0:P], ps[:, 4, 2 * P:3 * P], part[:, 0:1], part[:, 1:2],
                                  ALU.is_le, ALU.mult).then_inc(s_table, 1)

            def use_max(g, i, j):
                for u, (lo, width) in enumerate(a_units(i)):
                    n = a_no[("max", g, i, j, u)]
                    bank = ps[:, A_BANKS[n % 2], 0:width]
                    dve.wait_ge(s_ap, n + 1)
                    if lo + width == (i + 1) * P:
                        dve.tensor_tensor_reduce(bank, bank, mask_qk[:, 512 - width:512], 1.0, TAKEN,
                                                 ALU.add, ALU.max, mx[:, g % 2, j, i:i + 1]).then_inc(s_ad, 1)
                    else:
                        dve.reduce_max(mx_low[:, g % 2, j, i - 4:i - 3], bank, AX.X).then_inc(s_ad, 1)

            def use_neg(g):
                dve.wait_ge(s_ad, a_no[("neg", g)])
                dve.tensor_tensor(mx[:, g % 2, :, 4:8], mx[:, g % 2, :, 4:8], mx_low[:, g % 2, :, :],
                                  ALU.max).then_inc(s_mx, 1)
                n = a_no[("neg", g)]
                dve.wait_ge(s_ap, n + 1)
                bank = ps[0:HG * NT, A_BANKS[n % 2], 0:P]
                link(dve.tensor_scalar(neg_hi[:, g % 2, :], bank, -1.0, None, ALU.mult))
                dve.scalar_tensor_tensor(neg_lo[:, g % 2, :], bank, -1.0, neg_hi[:, g % 2, :].bitcast(F32),
                                         ALU.mult, ALU.subtract).then_inc(s_neg, 1)
                dve.wait_ge(s_neg, g + 1)
                dve.sem_inc(s_ad, 1)

            def use_post(g, q):
                n = a_no[("post", g, q)]
                dve.wait_ge(s_ap, n + 1)
                bank = ps[:, A_BANKS[n % 2], :].rearrange("p (t h c) -> p t h c", h=HG, c=VW)
                link(dve.reciprocal(rec[:, :, :].rearrange("p t (h a) -> p t h a", a=1), bank[:, :, :, DK:DK + 1]))
                dve.tensor_tensor(
                    att[:, 4 * q:4 * q + 4, g * HG * DK:(g + 1) * HG * DK].rearrange("p t (h c) -> p t h c", c=DK),
                    bank[:, :, :, 0:DK],
                    rec[:, :, :].rearrange("p t (h a) -> p t h a", a=1).to_broadcast([P, 4, HG, DK]),
                    ALU.mult).then_inc(s_att, 1)
                dve.wait_ge(s_att, 2 * g + q + 1)
                dve.sem_inc(s_ad, 1)

            for g in range(-1, G + 1):
                for kt in range(NT):
                    if kt == 2 and g >= 1:
                        use_post(g - 1, 0)
                        use_post(g - 1, 1)
                    for j in range(HG):
                        if g + 1 < G:
                            for i in A_STEPS[kt]:
                                use_max(g + 1, i, j)
                    if g == -1 and kt == 0:
                        count_and_map()
                    if g == 0 and kt == 0:
                        weights()
                    if g == 1 and kt == 0:
                        tile_columns()
                if g + 1 < G:
                    use_neg(g + 1)
            tables()

            for t in range(NT):
                dve.wait_ge(s_op, t + 1)
                dve.tensor_tensor(x_sb[:, t, :], ps[:, 2 + t % 2, 0:D], x_sb[:, t, :], ALU.add).then_inc(s_res, 1)

            dve.wait_ge(s_table, 1)
            more = dve.value_load(steps_i[0:1, 0:1], min_val=MIN_STEPS - 1, max_val=STEPS - 1)

            def meta(n, u, y, turn, added):
                dve.wait_ge(s_xg[u], 16 * turn + 16)
                wait_turn(dve, s_add[y], 16 * added)
                dve.scalar_tensor_tensor(w_junk[y][:, :], xg[u][:, EXP:EXP + K], tile_exp[:, bass.ds(n, 1)],
                                         xg[u][:, WGT:WGT + K], ALU.is_equal, ALU.mult, accum_out=w_slot[y][:, 0:1])
                dve.tensor_tensor(dst[y][:, 0:1], xg[u][:, TOK:TOK + 1], tile_out[:, bass.ds(n, 1)],
                                  ALU.max).then_inc(s_meta, 1)

            def rows_out(n, b):
                dve.wait_ge(s_T, n + 1)
                wait_turn(dve, s_gu, n - 1)
                dve.tensor_copy(xgT[b], ps[:, b, 0:DC * P]).then_inc(s_Te, 1)

            def hidden(n, b):
                dve.wait_ge(s_th, n + 1)
                dve.scalar_tensor_tensor(sg[b], th[b], 1.0, ps[0:I, 2 + b, 0:P],
                                         ALU.add, ALU.mult).then_inc(s_sg, 1)
                dve.wait_ge(s_sg, n + 1)
                wait_turn(dve, s_dn, n - 1)
                dve.tensor_tensor(hh[b], sg[b], ps[0:I, 2 + b, P:2 * P], ALU.mult).then_inc(s_h, 1)

            def step(s):
                for u in range(1, U + 1):
                    n = s * U + u
                    rows_out(n + 2, u % 2)
                    hidden(n, u % 2)
                    meta(n, u % U, u % NY, s + u // U, s * (U // NY) + u // NY)

            rows_out(0, 0)
            rows_out(1, 1)
            hidden(0, 0)
            meta(0, 0, 0, 0, 0)
            rows_out(2, 0)
            step(0)
            with dve.Fori(1, STEPS) as s:
                with dve.If(s <= more):
                    step(s)

            for j in range(NY):
                dve.wait_ge(s_yl[j], 16)
            a, b = slice(0, NT // 2), slice(NT // 2, NT)
            link(dve.tensor_tensor(sum_buf(0)[:, a], sum_buf(0)[:, a], sum_buf(1)[:, a], ALU.add))
            link(dve.tensor_tensor(sum_buf(0)[:, a], sum_buf(0)[:, a], sum_buf(2)[:, a], ALU.add))
            dve.tensor_tensor(sum_buf(0)[:, a], sum_buf(0)[:, a], sum_buf(3)[:, a], ALU.add).then_inc(s_fin[0], 1)
            link(dve.tensor_tensor(sum_buf(0)[:, b], sum_buf(0)[:, b], sum_buf(1)[:, b], ALU.add))
            dve.wait_ge(s_yp, 1)
            dve.tensor_tensor(sum_buf(0)[:, b], sum_buf(0)[:, b], sum_buf(2)[:, b], ALU.add).then_inc(s_fin[1], 1)


def kernel(**inputs):
    import numpy as np
    import concourse.bacc as bacc
    from concourse.bass_utils import run_bass_kernel_spmd

    f32 = np.float32
    inv = (f32(10000.0) ** (-(np.arange(0, DK, 2, dtype=f32) / f32(DK)))).astype(f32)
    ang = (np.arange(N, dtype=f32)[:, None] * inv).astype(f32)
    cos = np.repeat(np.cos(ang), 2, axis=1).astype(f32)
    sin = np.repeat(np.sin(ang), 2, axis=1).astype(f32) * np.tile(np.array([-1, 1], f32), DK // 2)

    def by_tile(a):
        return np.ascontiguousarray(a.reshape(NT, P, DK).transpose(1, 0, 2))

    a = {k: np.asarray(v) for k, v in inputs.items()}
    w_in = np.concatenate([a["L0_attn_wq"].T, a["L0_attn_wk"].T, a["L0_attn_wv"].T, a["L0_ffn_gate_weight"].T], 1)
    gu = np.concatenate([a["L0_ffn_w_gate"], a["L0_ffn_w_up"]], 2)
    gu = gu.reshape(E, DC, P, 2 * I).transpose(0, 2, 1, 3).reshape(E, P, DC * 2 * I)
    down = np.pad(a["L0_ffn_w_down"], ((0, 0), (0, P - I), (0, 0)))
    w_exp = np.concatenate([gu, down], 2)
    arrays = {
        "x": a["L0_attn_x"].reshape(N, D), "cos": by_tile(cos), "sin": by_tile(sin), "w_in": w_in,
        "w_out": a["L0_attn_wo"].T, "w_exp": w_exp,
    }
    arrays = {k: np.ascontiguousarray(v) for k, v in arrays.items()}
    nc = bacc.Bacc("TRN2", target_bir_lowering=False, num_devices=1)
    args = [nc.dram_tensor(k, v.shape, mybir.dt.from_np(v.dtype), kind="ExternalInput").ap() for k, v in arrays.items()]
    out = nc.dram_tensor("out", (N, D), F32, kind="ExternalOutput").ap()
    build(nc, *args, out)
    r = run_bass_kernel_spmd(nc, [arrays], core_ids=[0])
    return r.results[0]["out"].reshape(1, N, D)
```

```python
from contextlib import ExitStack

import concourse.bass as bass
from concourse import mybir

F32 = mybir.dt.float32
F32R = mybir.dt.float32r
BF16 = mybir.dt.bfloat16
I32 = mybir.dt.int32
U32 = mybir.dt.uint32
ALU = mybir.AluOpType
ACT = mybir.ActivationFunctionType
AX = mybir.AxisListType

P = 128
N = 1024
D = 256
NT = N // P
DC = D // P
H = 16
DK = D // H
HG = 4
G = H // HG
VW = 32
E = 64
K = 8
I = 96
ROW = D + 1 + 2 * K
TOK, EXP, WGT = D, D + 1, D + 1 + K
W_ROW = DC * 2 * I + D
MASKED = -1.0e30
TAKEN = -3.0e38
EPS = 1e-5
LN_FIRST = 2
PAIRS = N * K
U = 8
STEPS = (PAIRS // P + E) // U
MIN_STEPS = E // U
TILES = STEPS * U + U
NY = 4
BOUNDED = "the tables are made with first slots clamped to PAIRS and experts to E - 1"
B_BANKS, PV_BANK, A_BANKS = (0, 1, 2), 3, (5, 6, 7)
HALF = N // 2
CT = NT // 2
A_START = 6


def a_units(i):
    width = (i + 1) * P
    return [(0, width)] if width <= 512 else [(0, 512), (512, width - 512)]


def halves(kt):
    return [(max(kt * P, lo), lo + HALF) for lo in (0, HALF) if kt * P < lo + HALF]


def attention_order():
    jobs = [(i, j) for i in reversed(range(NT)) for j in range(HG)]
    at = {}
    for g in range(-1, G + 1):
        left, taken, passed = list(jobs), 0, 0
        work = HG * NT * (NT + 1) // 2
        skipped = sum(n // HG + 1 for n in range(A_START))
        for step in range(NT):
            for j in range(HG):
                here = at[(g, step, j)] = []
                passed += step + 1
                if step == 1 and j == 0 and g >= 0 and g < G:
                    here.append(("neg", g, 0))
                if step == 2 and j == 0 and g >= 1:
                    here += [("post", g - 1, q) for q in range(2)]
                if g + 1 >= G:
                    continue
                share = 1 if g < 0 else (passed - skipped) / (work - skipped - NT)
                while left and taken < share * work:
                    i, h = left.pop(0)
                    taken += i + 1
                    here += [("max", g + 1, i, h, u) for u in range(len(a_units(i)))]
                    if (i, h) == ((CT, HG - 1) if g < 0 else (CT - 1, 2)):
                        here.append(("neg", g + 1, 1))
    return at


def wait_turn(eng, semaphore, value):
    if not isinstance(value, int) or value > 0:
        eng.wait_ge(semaphore, value)


def build(nc, x, cos, sin, w_in, w_out, w_exp, out):
    ctx = ExitStack()
    with ctx:
        def sb(name, shape, dt=F32):
            return ctx.enter_context(nc.sbuf_tensor(name, shape, dt))

        def sem(name):
            return ctx.enter_context(nc.semaphore(name))

        def dram(name, shape, dt=F32):
            return nc.dram_tensor(name, shape, dt).ap()

        WIN = 3 * D + E
        qk_parts = dram("qk_parts", [2, 2 * D, N])
        slots = dram("slots", [PAIRS + P, ROW])
        y_acc = [dram(f"y_acc{j}", [N + P, D]) for j in range(NY)]

        x_sb = sb("x_sb", [P, NT, D])
        rows = sb("rows", [P, NT, ROW])
        cos_sb = sb("cos_sb", [P, NT, DK])
        sin_sb = sb("sin_sb", [P, NT, DK])
        w_in_sb = sb("w_in_sb", [P, DC, WIN])
        w_out_sb = sb("w_out_sb", [P, DC, D])
        ident = sb("ident", [P, P])
        ones = sb("ones", [P, P])
        ident_b = sb("ident_b", [P, P], BF16)
        ones_b = sb("ones_b", [P, P], BF16)
        zero_b = sb("zero_b", [P, P], BF16)
        before_b = sb("before_b", [P, P], BF16)
        mask_kq = sb("mask_kq", [P, P], BF16)
        mask_qk = sb("mask_qk", [P, 512], BF16)
        zero = sb("zero", [P, 3 * D])
        part = sb("part", [P, 2])
        stats = sb("stats", [P, NT, 6])
        moments = sb("moments", [P, NT, 2])
        rstd = sb("rstd", [P, NT])
        var_eps = sb("var_eps", [P, NT])
        minus_half = sb("minus_half", [P, NT])
        xnT = sb("xnT", [P, DC, N])
        rope_c = sb("rope_c", [P, 2, 2 * D])
        rope_s = sb("rope_s", [P, 2, 2 * D])
        qk_rot = sb("qk_rot", [P, 2, 2 * D])
        part_hi = sb("part_hi", [P, 2, 4 * P], F32R)
        part_lo = sb("part_lo", [P, 2, 4 * P], F32R)
        v_aug = sb("v_aug", [P, NT, H, VW])
        qz = sb("qz", [P, 2, 2, HG, HALF], F32R)
        kz = sb("kz", [P, 2, 2, HG, HALF], F32R)
        mx = sb("mx", [P, 2, 2, HG, CT])
        mx_low = sb("mx_low", [P, 2, HG, CT])
        neg_hi = sb("neg_hi", [HG * CT, 2, 2, P], F32R)
        neg_lo = sb("neg_lo", [HG * CT, 2, 2, P], F32R)
        probs = sb("probs", [P, 2, HG, N])
        att_raw = sb("att_raw", [P, N])
        rec = sb("rec", [P, 4, HG])
        att = sb("att", [P, NT, D])
        attT = probs[:, 0, 0:DC, :]
        logits = sb("logits", [P, NT, E])
        top_v = sb("top_v", [P, NT, K])
        top_i = sb("top_i", [P, NT, K], U32)
        replaced = sb("replaced", [P, NT, E])
        chosen = sb("chosen", [P, NT, E], BF16)
        top_d = sb("top_d", [P, NT, K])
        top_e = sb("top_e", [P, NT, K])
        top_s = sb("top_s", [P, NT])
        top_r = sb("top_r", [P, NT])
        slot_map = replaced
        slot_f = sb("slot_f", [P, NT, K])
        slot_i = sb("slot_i", [P, NT, K], I32)
        tok_i = sb("tok_i", [P, NT], I32)
        cnt = sb("cnt", [P, E])
        end_e = sb("end_e", [P, E])
        base_e = sb("base_e", [P, E])
        n_i = sb("n_i", [P, 2, E], I32)
        n_e = sb("n_e", [P, E])
        t_end = sb("t_end", [P, E])
        t_beg = sb("t_beg", [P, E])
        shift_e = sb("shift_e", [P, E])
        is_le = sb("is_le", [P, 2, E])
        hot = sb("hot", [P, E])
        junk_e = sb("junk_e", [P, 2, E])
        col = sb("col", [P, 6])
        spread = sb("spread", [P, 3, P])
        tile_row = sb("tile_row", [1, 2 * TILES], I32)
        tile_exp = sb("tile_exp", [P, TILES])
        tile_out = sb("tile_out", [P, TILES])
        steps_f = sb("steps_f", [P, 1], I32)
        steps_i = sb("steps_i", [P, 1], I32)
        def part_of(flat, n, width, rows_=P):
            return flat[0:rows_, n * width:(n + 1) * width]

        v_flat = v_aug[:, :, :, :].rearrange("p t h c -> p (t h c)")
        probs_flat = probs[:, :, :, :].rearrange("p b h n -> p (b h n)")
        rope_s_flat = rope_s[:, :, :].rearrange("p b n -> p (b n)")
        qk_rot_flat = qk_rot[:, :, :].rearrange("p b n -> p (b n)")
        xg = [part_of(v_flat, u, ROW) for u in range(U)]
        w_all = [part_of(probs_flat, u, W_ROW) for u in range(U)]
        wgu = [w[:, 0:DC * 2 * I].rearrange("p (c i) -> p c i", c=DC) for w in w_all]
        wdn = [w[0:I, DC * 2 * I:W_ROW] for w in w_all]
        y_sb = [part_of(rope_s_flat, u, D) for u in range(NY)]
        xgT = [part_of(qk_rot_flat, u, D) for u in range(2)]
        th = [part_of(qk_rot_flat, 4 + u, P, I) for u in range(2)]
        sg = [part_of(qk_rot_flat, 6 + u, P, I) for u in range(2)]
        hidden_sb = sb("hidden_sb", [I, 2 * P])
        hh = [hidden_sb[:, u * P:(u + 1) * P] for u in range(2)]
        w_junk = [sb(f"w_junk{u}", [P, K]) for u in range(NY)]
        w_slot = [sb(f"w_slot{u}", [P, 1]) for u in range(NY)]
        dst = [sb(f"dst{u}", [P, 1], I32) for u in range(NY)]

        ps = ctx.enter_context(nc.psum_tensor("ps", [P, 8, 512], F32))

        s_x = [sem(f"x_loaded{t}") for t in range(NT)]
        s_w = sem("weights_loaded")
        s_const = sem("constants_ready")
        s_pchain = sem("pool_chain")
        s_vchain = sem("vector_chain")
        s_zero = sem("zeros_ready")
        s_clear = sem("spare_rows_set")
        s_zeroed = sem("scratch_zeroed")
        s_var = sem("variances_ready")
        s_rstd = sem("rstd_ready")
        s_ident = sem("identity_ready")
        s_xn = sem("rows_normalised")
        s_xT = sem("rows_transposed")
        s_xTe = sem("xnT_ready")
        s_proj = sem("projected")
        s_vlog = sem("v_and_logits_out")
        s_rope = sem("rope_products")
        s_rot = sem("qk_rotated")
        s_qkT = sem("qk_transposed")
        s_hi = sem("hi_ready")
        s_lo = sem("lo_ready")
        s_parts = [sem(f"parts_stored{b}") for b in range(2)]
        s_sq = [[sem(f"q_staged{b}{c}") for c in range(2)] for b in range(2)]
        s_sk = [[sem(f"k_staged{b}{c}") for c in range(2)] for b in range(2)]
        s_ap = sem("a_unit_made")
        s_ad = sem("a_unit_used")
        s_mx = sem("maxima_ready")
        s_neg = sem("negmax_ready")
        s_negd = [[sem(f"negmax_placed{b}{c}") for c in range(2)] for b in range(2)]
        s_bp = sem("scores_made")
        s_be = sem("probs_ready")
        s_pv = sem("pv_done")
        s_acc = sem("att_out")
        s_att = sem("att_normalised")
        s_aT = sem("att_transposed")
        s_aTe = sem("attT_ready")
        s_op = sem("out_projected")
        s_res = sem("residual_ready")
        s_resd = sem("residual_stored")
        s_chosen = sem("chosen_ready")
        s_d = sem("top_differences")
        s_e = sem("top_exponentials")
        s_route = sem("rows_complete")
        s_cnt = sem("counts_made")
        s_smap = sem("counts_used")
        s_sloti = sem("slot_numbers")
        s_scat = sem("rows_scattered")
        s_spread = sem("tile_columns")
        s_spread2 = sem("tile_columns_spread")
        s_table = sem("tile_tables")
        s_xg = [sem(f"tile_rows{u}") for u in range(U)]
        s_wt = [sem(f"tile_weights{u}") for u in range(U)]
        s_T = sem("tile_transposed")
        s_Te = sem("tile_xT_ready")
        s_gu = sem("tile_gate_up")
        s_th = sem("tile_tanh")
        s_sg = sem("tile_silu")
        s_h = sem("tile_hidden")
        s_dn = sem("tile_down")
        s_meta = sem("tile_destinations")
        s_y = sem("tile_result")
        s_add = [sem(f"tile_added{u}") for u in range(NY)]
        s_yl = [sem(f"sums_loaded{j}") for j in range(NY)]
        s_yp = sem("partial_sum")
        s_turn = sem("tile_may_be_added")
        s_all = sem("all_added")
        s_fin = [sem(f"final_sum{i}") for i in range(2)]
        s_out = sem("stored")

        CONSTS = 9

        a_at = attention_order()
        a_order = [unit for units in a_at.values() for unit in units]
        a_no = {unit: n for n, unit in enumerate(a_order)}

        def a_bank(unit):
            return ps[:, A_BANKS[a_no[unit] % len(A_BANKS)], :]

        b_order = [(g, kt, j, lo) for g in range(G) for kt in reversed(range(NT)) for j in range(HG)
                   for lo, _ in halves(kt)]
        b_numbers = {unit: n for n, unit in enumerate(b_order)}

        def b_no(g, kt, j, lo=None):
            return b_numbers[(g, kt, j, halves(kt)[-1][0] if lo is None else lo)]

        def head_rows(tile, g, j, tile_no, rows_):
            c, t = divmod(tile_no, CT)
            return tile[0:rows_, g % 2, c, j, t * P:(t + 1) * P]

        def sum_buf(j):
            return probs[:, j // 2, 2 * (j % 2):2 * (j % 2) + 2, :].rearrange("p a (t d) -> p (a t) d", d=D)

        block = ctx.enter_context(nc.Block())

        @block.sync
        def _(sp):
            xv = x.rearrange("(t p) d -> t p d", p=P)
            for t in range(NT):
                sp.dma_start(x_sb[:, t, :], xv[t]).then_inc(s_x[t], 16)
            sp.wait_ge(s_zero, 2)
            for b in range(2):
                for tile, lo, hi, src in ((qz, 64, P, zero), (kz, 64, 96, zero), (kz, 96, 98, ones), (kz, 98, P, zero)):
                    sp.dma_start(tile[lo:hi, b].bitcast(F32).rearrange("p c h (a n) -> p (c h a) n", n=P),
                                 src[lo:hi, 0:P].rearrange("p (a n) -> p a n", a=1)
                                 .to_broadcast([hi - lo, HG * NT, P])).then_inc(s_clear, 16)
            for j in range(NY):
                for r in range(0, N + P, 3 * P):
                    sp.dma_start(y_acc[j][r:r + 3 * P, :].rearrange("(p a) d -> p (a d)", a=3),
                                 zero[:, :]).then_inc(s_zeroed, 16)
            sp.dma_start(slots[PAIRS:PAIRS + P, :], zero[:, 0:ROW]).then_inc(s_zeroed, 16)
            def store_parts(t):
                for w, (tile, ready) in enumerate(((part_hi, s_hi), (part_lo, s_lo))):
                    sp.wait_ge(ready, t + 1)
                    sp.dma_start(qk_parts[w].rearrange("(b p) n -> p b n", p=P)[:, :, t * P:(t + 1) * P],
                                 tile[:, t % 2, :].bitcast(F32).rearrange("p (b n) -> p b n", n=P),
                                 ).then_inc(s_parts[t % 2], 16)

            def stage_k(g, c):
                f, n = D + g * HG * DK, slice(c * HALF, (c + 1) * HALF)
                for r, w in ((0, 0), (16, 1), (32, 1), (48, 0)):
                    sp.dma_start(kz[r:r + DK, g % 2, c, :, :].bitcast(F32),
                                 qk_parts[w, f:f + HG * DK, n].rearrange("(j f) n -> f j n", j=HG),
                                 ).then_inc(s_sk[g % 2][c], 16)

            def stage_q(g, c):
                f, n = g * HG * DK, slice(c * HALF, (c + 1) * HALF)
                for r, w in ((0, 0), (16, 1), (32, 0), (48, 1)):
                    sp.dma_start(qz[r:r + DK, g % 2, c, :, :].bitcast(F32),
                                 qk_parts[w, f:f + HG * DK, n].rearrange("(j f) n -> f j n", j=HG),
                                 ).then_inc(s_sq[g % 2][c], 16)

            def place_negmax(g, c):
                sp.wait_ge(s_neg, 2 * g + 2 - c)
                if g < 2:
                    sp.wait_ge(s_clear, 16 * 8)
                for r, src in ((96, neg_hi), (97, neg_lo)):
                    sp.dma_start(qz[r:r + 1, g % 2, c, :, :].bitcast(F32).rearrange("o h (i q) -> o (h i) q", q=P),
                                 src[:, g % 2, c, :].bitcast(F32)).then_inc(s_negd[g % 2][c], 16)

            for t in range(NT):
                store_parts(t)
                if t == CT:
                    for b in range(2):
                        sp.wait_ge(s_parts[b], 16 * CT)
                    stage_k(0, 0)
            for b in range(2):
                sp.wait_ge(s_parts[b], 16 * NT)
            stage_q(0, 1)
            stage_k(0, 1)
            stage_q(0, 0)
            for c in (1, 0):
                stage_k(1, c)
                stage_q(1, c)
            for c in (1, 0):
                place_negmax(0, c)
            for g in range(G - 1):
                if g + 2 < G:
                    sp.wait_ge(s_bp, b_no(g, CT, HG - 1) + 1)
                    stage_k(g + 2, 1)
                place_negmax(g + 1, 1)
                if g + 2 < G:
                    sp.wait_ge(s_bp, b_no(g, 0, HG - 1) + 1)
                    stage_q(g + 2, 1)
                    stage_k(g + 2, 0)
                    stage_q(g + 2, 0)
                place_negmax(g + 1, 0)

            sp.wait_ge(s_zeroed, 16 * (3 * NY + 1))
            sp.wait_ge(s_res, NT)
            sp.dma_start(y_acc[0][0:N, :].rearrange("(t p) d -> p t d", p=P), x_sb[:, :, :]).then_inc(s_resd, 16)

            sp.wait_ge(s_table, 1)
            sp.wait_ge(s_scat, 16 * NT * K)
            sp.wait_ge(s_pv, G * NT)
            more = sp.value_load(steps_i[0:1, 0:1], min_val=MIN_STEPS - 1, max_val=STEPS - 1)

            def numbers(turn):
                _, v = nc.values_load_multi_w_load_instructions(
                    tile_row[0:1, bass.ds(turn * (2 * U), 2 * U)], engines=[mybir.EngineType.SP],
                    min_val=0, max_val=PAIRS, skip_runtime_bounds_check_because=BOUNDED)
                return [(v[2 * u], nc.s_assert_within(v[2 * u + 1], 0, E - 1,
                                                      skip_runtime_bounds_check_because=BOUNDED)) for u in range(U)]

            def load(first, expert, u, last):
                if last is not None:
                    sp.wait_ge(s_T, last + 1)
                    sp.wait_ge(s_meta, last + 1)
                sp.dma_start(xg[u], slots[bass.ds(first, P), :]).then_inc(s_xg[u], 16)
                if last is not None:
                    sp.wait_ge(s_dn, last + 1)
                sp.dma_start(w_all[u], w_exp[bass.ds(expert, 1), :, :].rearrange("a p i -> (a p) i")).then_inc(s_wt[u], 16)

            for u, (first, expert) in enumerate(numbers(0)):
                load(first, expert, u, None)
            with sp.Fori(0, STEPS) as s:
                with sp.If(s <= more):
                    for u, (first, expert) in enumerate(numbers(s + 1)):
                        load(first, expert, u, s * U + u)

            for u in range(U):
                sp.wait_ge(s_xg[u], more * 16 + 32)
                sp.wait_ge(s_wt[u], more * 16 + 32)
            for j in range(NY):
                sp.wait_ge(s_all, 1)
                sp.dma_start(sum_buf(j), y_acc[j][0:N, :].rearrange("(t p) d -> p t d", p=P)).then_inc(s_yl[j], 16)
            sp.wait_ge(s_fin[0], 1)
            sp.dma_start(out.rearrange("(t p) d -> p t d", p=P)[:, 0:NT // 2, :], sum_buf(0)[:, 0:NT // 2, :]).then_inc(s_out, 16)
            sp.wait_ge(s_fin[1], 1)
            sp.dma_start(out.rearrange("(t p) d -> p t d", p=P)[:, NT // 2:NT, :], sum_buf(0)[:, NT // 2:NT, :]).then_inc(s_out, 16)
            sp.wait_ge(s_resd, 16)
            sp.wait_ge(s_out, 32)

        @block.gpsimd
        def _(pool):
            chained = [0]

            def link(ins):
                chained[0] += 1
                ins.then_inc(s_pchain, 1)
                pool.wait_ge(s_pchain, chained[0])

            link(pool.memset(ident[:, :], 0.0))
            pool.affine_select(out=ident[:, :], in_=ident[:, :], compare_op=ALU.not_equal, fill=1.0, base=0,
                               pattern=[[-1, P]], channel_multiplier=1).then_inc(s_ident, 1)
            pool.memset(zero[:, :], 0.0).then_inc(s_zero, 1)
            pool.memset(ones[:, :], 1.0).then_inc(s_zero, 1)
            link(pool.memset(minus_half[:, :], -0.5))
            for n, (lo, hi) in enumerate(((0, LN_FIRST), (LN_FIRST, NT))):
                pool.wait_ge(s_var, hi)
                pool.tensor_tensor(rstd[:, lo:hi], var_eps[:, lo:hi], minus_half[:, lo:hi], ALU.pow).then_inc(s_rstd, 1)
            link(pool.memset(ident_b[:, :], 0.0))
            pool.affine_select(out=ident_b[:, :], in_=ident_b[:, :], compare_op=ALU.not_equal, fill=1.0, base=0,
                               pattern=[[-1, P]], channel_multiplier=1).then_inc(s_const, 1)
            pool.memset(ones_b[:, :], 1.0).then_inc(s_const, 1)
            pool.memset(zero_b[:, :], 0.0).then_inc(s_const, 1)
            link(pool.memset(before_b[:, :], 1.0))
            pool.affine_select(out=before_b[:, :], in_=before_b[:, :], compare_op=ALU.is_gt, fill=0.0, base=0,
                               pattern=[[1, P]], channel_multiplier=-1).then_inc(s_const, 1)
            link(pool.memset(mask_kq[:, :], 0.0))
            pool.affine_select(out=mask_kq[:, :], in_=mask_kq[:, :], compare_op=ALU.is_ge, fill=MASKED, base=0,
                               pattern=[[1, P]], channel_multiplier=-1).then_inc(s_const, 1)
            link(pool.memset(mask_qk[:, :], 0.0))
            pool.affine_select(out=mask_qk[:, :], in_=mask_qk[:, :], compare_op=ALU.is_ge, fill=MASKED, base=512 - P,
                               pattern=[[-1, 512]], channel_multiplier=1).then_inc(s_const, 1)
            pool.iota(tok_i[:, :], [[P, NT]], base=0, channel_multiplier=1).then_inc(s_const, 1)
            pool.iota(part[:, :], [[N, 2]], base=0, channel_multiplier=1,
                      allow_small_or_imprecise_dtypes=True).then_inc(s_const, 1)
            link(pool.memset(v_aug[:, :, :, DK:VW], 0.0))
            pool.memset(v_aug[:, :, :, DK:DK + 1], 1.0).then_inc(s_const, 1)

            for t in range(NT):
                pool.wait_ge(s_rope, 3 * (t + 1))
                if t >= 2:
                    pool.wait_ge(s_qkT, t - 1)
                pool.tensor_tensor(qk_rot[:, t % 2, :], rope_c[:, t % 2, :], rope_s[:, t % 2, :],
                                   ALU.add).then_inc(s_rot, 1)

            pool.wait_ge(s_route, 1)
            pool.wait_ge(s_sloti, 1)
            for t in range(NT):
                for k in range(K):
                    pool.indirect_dma_start(slots[:, :], bass.IndirectOffsetOnAxis(ap=slot_i[:, t, k:k + 1], axis=0),
                                            rows[:, t, :], None).then_inc(s_scat, 16)

            pool.wait_ge(s_resd, 16)
            pool.wait_ge(s_zeroed, 16 * (3 * NY + 1))

            def add(n, u, before):
                pool.wait_ge(s_y, n + 1)
                wait_turn(pool, s_add[u], 16 * before)
                pool.sem_inc(s_turn, 1)
                pool.indirect_dma_start(y_acc[u][:, :], bass.IndirectOffsetOnAxis(ap=dst[u][:, 0:1], axis=0),
                                        y_sb[u], None, compute_op=ALU.add).then_inc(s_add[u], 16)

            more = pool.value_load(steps_i[0:1, 0:1], min_val=MIN_STEPS - 1, max_val=STEPS - 1)

            def step(s):
                for u in range(1, U + 1):
                    add(s * U + u, u % NY, s * (U // NY) + u // NY)

            add(0, 0, 0)
            step(0)
            with pool.Fori(1, STEPS) as s:
                with pool.If(s <= more):
                    step(s)
            pool.wait_ge(s_add[0], more * (16 * U // NY) + 16 * U // NY + 16)
            for u in range(1, NY):
                pool.wait_ge(s_add[u], more * (16 * U // NY) + 16 * U // NY)
            pool.sem_inc(s_all, 1)
            for j in range(NY):
                pool.wait_ge(s_yl[j], 16)
            h = slice(NT // 2, NT)
            link(pool.tensor_tensor(sum_buf(2)[:, h], sum_buf(2)[:, h], sum_buf(3)[:, h], ALU.add))
            pool.drain().then_inc(s_yp, 1)

        @block.scalar
        def _(act):
            act.dma_start(cos_sb[:, :, :], cos).then_inc(s_w, 16)
            act.dma_start(sin_sb[:, :, :], sin).then_inc(s_w, 16)
            act.dma_start(w_in_sb[:, :, :], w_in.rearrange("(c p) n -> p c n", p=P)).then_inc(s_w, 16)
            act.dma_start(w_out_sb[:, :, :], w_out.rearrange("(c p) n -> p c n", p=P)).then_inc(s_w, 16)

            def xT_out(t):
                act.wait_ge(s_xT, t + 1)
                act.activation(xnT[:, :, t * P:(t + 1) * P],
                               ps[:, t % 2, 0:DC * P].rearrange("p (c n) -> p c n", n=P), ACT.Copy).then_inc(s_xTe, 1)

            def v_out(t):
                act.wait_ge(s_proj, t + 1)
                act.activation(v_aug[:, t, :, 0:DK], ps[:, 4 + t % 2, 0:D].rearrange("p (h c) -> p h c", c=DK), ACT.Copy)
                act.activation(logits[:, t, :], ps[:, 4 + t % 2, D:D + E], ACT.Copy).then_inc(s_vlog, 1)

            def hi_out(t):
                act.wait_ge(s_qkT, t + 1)
                if t >= 2:
                    act.wait_ge(s_parts[t % 2], 32 * (t // 2))
                act.activation(part_hi[:, t % 2, :], ps[:, 6 + t % 2, :], ACT.Copy).then_inc(s_hi, 1)

            xT_out(0)
            for t in range(NT):
                if t + 1 < NT:
                    xT_out(t + 1)
                v_out(t)
                if t >= 1:
                    hi_out(t - 1)
            hi_out(NT - 1)

            def exps(g, step, j):
                kt = NT - 1 - step
                if step >= 2 or g > 0:
                    act.wait_ge(s_pv, g * NT + step - 1)
                for lo, hi in halves(kt):
                    n = b_no(g, kt, j, lo)
                    act.wait_ge(s_bp, n + 1)
                    act.activation(probs[:, step % 2, j, lo:hi],
                                   ps[:, B_BANKS[n % len(B_BANKS)], lo % HALF:(hi - 1) % HALF + 1],
                                   ACT.Exp, scale=DK ** -0.5).then_inc(s_be, 1)

            def att_out(g):
                act.wait_ge(s_pv, (g + 1) * NT)
                if g >= 1:
                    act.wait_ge(s_ap, a_no[("post", g - 1, 1)] + 1)
                act.activation(att_raw[:, :], ps[:, PV_BANK:PV_BANK + 2, :].rearrange("p a b -> p (a b)"),
                               ACT.Copy).then_inc(s_acc, 1)

            for g in range(G):
                for step in range(NT):
                    for j in range(HG):
                        exps(g, step, j)
                    if g == 0 and step == 0:
                        act.wait_ge(s_d, 1)
                        act.activation(top_e[:, :, :], top_d[:, :, :], ACT.Exp).then_inc(s_e, 1)
                    if g > 0 and step == 0:
                        att_out(g - 1)
            att_out(G - 1)
            for t in range(NT):
                act.wait_ge(s_aT, t + 1)
                act.activation(attT[:, :, t * P:(t + 1) * P],
                               ps[:, t % 2, 0:DC * P].rearrange("p (c n) -> p c n", n=P), ACT.Copy).then_inc(s_aTe, 1)

            act.wait_ge(s_table, 1)
            more = act.value_load(steps_i[0:1, 0:1], min_val=MIN_STEPS - 1, max_val=STEPS - 1)

            def tanh(n, b):
                act.wait_ge(s_gu, n + 1)
                wait_turn(act, s_h, n - 1)
                act.activation(th[b], ps[0:I, 2 + b, 0:P], ACT.Tanh, scale=0.5).then_inc(s_th, 1)

            def result(n, u, b, added):
                act.wait_ge(s_dn, n + 1)
                act.wait_ge(s_meta, n + 1)
                wait_turn(act, s_add[u], 16 * added)
                act.activation(y_sb[u], ps[:, 4 + b, 0:D], ACT.Copy, scale=w_slot[u][:, 0:1]).then_inc(s_y, 1)

            def step(s):
                for u in range(1, U + 1):
                    n = s * U + u
                    tanh(n, u % 2)
                    result(n - 1, (u - 1) % NY, (u - 1) % 2, s * (U // NY) + (u - 1) // NY)

            tanh(0, 0)
            step(0)
            with act.Fori(1, STEPS) as s:
                with act.If(s <= more):
                    step(s)
            result(more * U + U, 0, 0, more * (U // NY) + U // NY)

        @block.tensor
        def _(pe):
            def x_transpose(t):
                pe.wait_ge(s_xn, t + 1)
                if t >= 2:
                    pe.wait_ge(s_xTe, t - 1)
                for c in range(DC):
                    last = pe.transpose(ps[:, t % 2, c * P:(c + 1) * P], rows[:, t, c * P:(c + 1) * P], ident[:, :])
                last.then_inc(s_xT, 1)

            def project(t):
                pe.wait_ge(s_xTe, t + 1)
                if t >= 2:
                    pe.wait_ge(s_rope, 3 * (t - 1))
                    pe.wait_ge(s_vlog, t - 1)
                for bank, lo, hi in ((4, 2 * D, WIN), (2, 0, 2 * D)):
                    for c in range(DC):
                        last = pe.matmul(ps[:, bank + t % 2, 0:hi - lo], xnT[:, c, t * P:(t + 1) * P],
                                         w_in_sb[:, c, lo:hi], start=(c == 0), stop=(c == DC - 1))
                last.then_inc(s_proj, 1)

            def qk_transpose(t):
                pe.wait_ge(s_rot, t + 1)
                if t >= 2:
                    pe.wait_ge(s_lo, t - 1)
                for b in range(4):
                    last = pe.transpose(ps[:, 6 + t % 2, b * P:(b + 1) * P], qk_rot[:, t % 2, b * P:(b + 1) * P],
                                        ident[:, :])
                last.then_inc(s_qkT, 1)

            pe.wait_ge(s_ident, 1)
            x_transpose(0)
            pe.wait_ge(s_w, 64)
            for t in range(NT):
                if t + 1 < NT:
                    x_transpose(t + 1)
                project(t)
                if t >= 1:
                    qk_transpose(t - 1)
            qk_transpose(NT - 1)

            pe.wait_ge(s_const, CONSTS)
            pe.wait_ge(s_chosen, 1)
            pe.wait_ge(s_vlog, NT)
            pe.wait_ge(s_rope, 3 * NT)
            for t in range(NT):
                pe.matmul(ps[:, 3, 0:E], ones_b[:, :], chosen[:, t, :], start=(t == 0), stop=(t == NT - 1))
            for t in range(NT):
                for s in range(t + 1):
                    last = pe.matmul(ps[:, 4, t * E:(t + 1) * E], before_b[:, :] if s == t else ones_b[:, :],
                                     chosen[:, s, :], start=(s == 0), stop=(s == t))
            last.then_inc(s_cnt, 1)

            def a_free(unit):
                n = a_no[unit]
                if n >= len(A_BANKS):
                    pe.wait_ge(s_ad, n - len(A_BANKS) + 1)
                elif n == 0:
                    pe.wait_ge(s_lo, NT)
                return a_bank(unit)

            def max_scores(g, i, j, u):
                lo, width = a_units(i)[u]
                bank = a_free(("max", g, i, j, u))
                pe.matmul(bank[:, 0:width], head_rows(qz, g, j, i, 96), kz[0:96, g % 2, lo // HALF, j, 0:width],
                          start=True, stop=True).then_inc(s_ap, 1)

            def neg_transpose(g, c):
                bank = a_free(("neg", g, c))
                if c == 1:
                    pe.wait_ge(s_mx, g + 1)
                else:
                    pe.wait_ge(s_ad, a_no[("max", g, 0, HG - 1, 0)] + 1)
                pe.transpose(bank[0:HG * CT, 0:P], mx[:, g % 2, c, :, :].rearrange("p h i -> p (h i)"),
                             ident[:, :]).then_inc(s_ap, 1)

            def scores(g, kt, j):
                for lo, hi in halves(kt):
                    n = b_no(g, kt, j, lo)
                    if n >= len(B_BANKS):
                        pe.wait_ge(s_be, n - len(B_BANKS) + 1)
                    else:
                        pe.wait_ge(s_rope, 3 * NT)
                    a, b = lo % HALF, (hi - 1) % HALF + 1
                    bank = ps[:, B_BANKS[n % len(B_BANKS)], :]
                    last = pe.matmul(bank[:, a:b], head_rows(kz, g, j, kt, P), qz[:, g % 2, lo // HALF, j, a:b],
                                     start=True, stop=True, skip_group_check=True)
                    if lo == kt * P:
                        last = pe.matmul(bank[:, a:a + P], ident_b[:, :], mask_kq[:, :], start=False, stop=True,
                                         skip_group_check=True)
                    last.then_inc(s_bp, 1)

            def pv(g, step, half):
                kt = NT - 1 - step
                if half == 0:
                    pe.wait_ge(s_be, b_no(g, kt, HG - 1) + 1)
                    if step == 0:
                        if g >= 1:
                            pe.wait_ge(s_acc, g)
                        for b in range(2):
                            pe.matmul(ps[:, PV_BANK + b, :], zero_b[:, :], mask_qk[:, :], start=True, stop=True)
                ranges = halves(kt)
                last = None
                if half == 0 or len(ranges) == 2:
                    lo, hi = ranges[-1 - half]
                    for j in range(HG):
                        last = pe.matmul(ps[VW * j:VW * (j + 1), PV_BANK + lo // HALF, lo % HALF:(hi - 1) % HALF + 1],
                                         v_aug[:, kt, g * HG + j, :], probs[:, step % 2, j, lo:hi],
                                         start=False, stop=True, skip_group_check=True)
                if half == len(ranges) - 1:
                    last.then_inc(s_pv, 1)

            def post(g, q):
                bank = a_free(("post", g, q))
                pe.wait_ge(s_acc, g + 1)
                for t in range(4):
                    last = pe.transpose(bank[:, t * P:(t + 1) * P], att_raw[:, (4 * q + t) * P:(4 * q + t + 1) * P],
                                        ident[:, :])
                last.then_inc(s_ap, 1)

            make = {"max": max_scores, "neg": neg_transpose, "post": post}
            pe.wait_ge(s_clear, 16 * 8)
            for g in range(-1, G + 1):
                for step in range(NT):
                    kt = NT - 1 - step
                    if step == 0 and 0 <= g < G:
                        pe.wait_ge(s_negd[g % 2][1], 32 * (g // 2 + 1))
                    if kt == CT - 1 and 0 <= g < G:
                        pe.wait_ge(s_negd[g % 2][0], 32 * (g // 2 + 1))
                    if step == 0 and g == 0:
                        pe.wait_ge(s_smap, 1)
                    for j in range(HG):
                        if 0 <= g < G:
                            scores(g, kt, j)
                        for kind, *what in a_at[(g, step, j)]:
                            if kind == "max" and what[1:] == [NT - 1, 0, 0]:
                                for c in range(2):
                                    pe.wait_ge(s_sq[what[0] % 2][c], 64 * (what[0] // 2 + 1))
                                    pe.wait_ge(s_sk[what[0] % 2][c], 64 * (what[0] // 2 + 1))
                            make[kind](*what)
                        if j % 2 == 1 and 0 <= g < G and step >= 1:
                            pv(g, step - 1, j // 2)
                        if j % 2 == 1 and g >= 1 and step == 0:
                            pv(g - 1, NT - 1, j // 2)

            pe.wait_ge(s_spread, 1)
            pe.matmul(ps[:, 4, 0:3 * P], ones[:, :], spread[:, :, :].rearrange("p a b -> p (a b)"),
                      start=True, stop=True).then_inc(s_spread2, 1)

            pe.wait_ge(s_att, 2 * G)
            for t in range(NT + 1):
                if t < NT:
                    if t >= 2:
                        pe.wait_ge(s_aTe, t - 1)
                    for c in range(DC):
                        last = pe.transpose(ps[:, t % 2, c * P:(c + 1) * P], att[:, t, c * P:(c + 1) * P], ident[:, :])
                    last.then_inc(s_aT, 1)
                if t >= 1:
                    o = t - 1
                    pe.wait_ge(s_aTe, o + 1)
                    if o >= 2:
                        pe.wait_ge(s_res, o - 1)
                    for c in range(DC):
                        last = pe.matmul(ps[:, 2 + o % 2, 0:D], attT[:, c, o * P:(o + 1) * P], w_out_sb[:, c, :],
                                         start=(c == 0), stop=(c == DC - 1))
                    last.then_inc(s_op, 1)

            pe.wait_ge(s_aTe, NT)
            pe.wait_ge(s_res, NT)
            pe.wait_ge(s_table, 1)
            more = pe.value_load(steps_i[0:1, 0:1], min_val=MIN_STEPS - 1, max_val=STEPS - 1)

            def transpose_rows(n, u, b, turn):
                pe.wait_ge(s_xg[u], 16 * turn + 16)
                wait_turn(pe, s_Te, n - 1)
                for c in range(DC):
                    last = pe.transpose(ps[:, b, c * P:(c + 1) * P], xg[u][:, c * P:(c + 1) * P], ident[:, :])
                last.then_inc(s_T, 1)

            def gate_up(n, u, b, turn):
                pe.wait_ge(s_Te, n + 1)
                pe.wait_ge(s_wt[u], 16 * turn + 16)
                wait_turn(pe, s_h, n - 1)
                for w in range(2):
                    for c in range(DC):
                        last = pe.matmul(ps[0:I, 2 + b, w * P:(w + 1) * P], wgu[u][:, c, w * I:(w + 1) * I],
                                         xgT[b][:, c * P:(c + 1) * P], start=(c == 0), stop=(c == DC - 1))
                last.then_inc(s_gu, 1)

            def down(n, u, b):
                pe.wait_ge(s_h, n + 1)
                pe.matmul(ps[:, 4 + b, 0:D], hh[b], wdn[u], start=True, stop=True).then_inc(s_dn, 1)

            def step(s):
                for u in range(1, U + 1):
                    n = s * U + u
                    gate_up(n, u % U, u % 2, s + u // U)
                    transpose_rows(n + 2, (u + 2) % U, u % 2, s + (u + 2) // U)
                    down(n - 1, (u - 1) % U, (u - 1) % 2)
                    wait_turn(pe, s_y, n - 1)

            transpose_rows(0, 0, 0, 0)
            transpose_rows(1, 1, 1, 0)
            gate_up(0, 0, 0, 0)
            transpose_rows(2, 2, 0, 0)
            step(0)
            with pe.Fori(1, STEPS) as s:
                with pe.If(s <= more):
                    step(s)
            down(more * U + U, 0, 0)

        @block.vector
        def _(dve):
            chained = [0]

            def link(ins):
                chained[0] += 1
                ins.then_inc(s_vchain, 1)
                dve.wait_ge(s_vchain, chained[0])

            def measure(t):
                dve.wait_ge(s_x[t], 16)
                link(dve.bn_stats(stats[:, t, :], x_sb[:, t, :]))
                link(dve.bn_aggr(moments[:, t, :], stats[:, t, :]))
                dve.tensor_scalar(var_eps[:, t:t + 1], moments[:, t, 1:2], EPS, None, ALU.add).then_inc(s_var, 1)

            def normalise(t):
                dve.wait_ge(s_rstd, 1 if t < LN_FIRST else 2)
                dve.tensor_scalar(rows[:, t, 0:D], x_sb[:, t, :], moments[:, t, 0:1], rstd[:, t:t + 1],
                                  ALU.subtract, ALU.mult).then_inc(s_xn, 1)

            def rotate(t):
                dve.wait_ge(s_proj, t + 1)
                if t >= 2:
                    dve.wait_ge(s_rot, t - 1)
                heads = 2 * D // DK
                qk = ps[:, 2 + t % 2, :].rearrange("p (h c) -> p h c", c=DK)

                def table(tab):
                    return tab[:, t, :].rearrange("p (a c) -> p a c", a=1).to_broadcast([P, heads, DK])

                dve.tensor_tensor(rope_c[:, t % 2, :].rearrange("p (h c) -> p h c", c=DK), qk, table(cos_sb),
                                  ALU.mult).then_inc(s_rope, 1)
                for odd in range(2):
                    dve.tensor_tensor(rope_s[:, t % 2, :].rearrange("p (h c) -> p h c", c=DK)[:, :, odd::2],
                                      qk[:, :, 1 - odd::2], table(sin_sb)[:, :, odd::2], ALU.mult).then_inc(s_rope, 1)

            def lo_out(t):
                dve.wait_ge(s_hi, t + 1)
                if t >= 2:
                    dve.wait_ge(s_parts[t % 2], 32 * (t // 2))
                dve.tensor_tensor(part_lo[:, t % 2, :], ps[:, 6 + t % 2, :], part_hi[:, t % 2, :].bitcast(F32),
                                  ALU.subtract).then_inc(s_lo, 1)

            for t in range(NT):
                measure(t)
                if t == LN_FIRST:
                    for first in range(LN_FIRST):
                        normalise(first)
            normalise(LN_FIRST)
            dve.wait_ge(s_w, 64)
            for t in range(NT):
                rotate(t)
                if t + LN_FIRST + 1 < NT:
                    normalise(t + LN_FIRST + 1)
                if t >= 1:
                    lo_out(t - 1)
            lo_out(NT - 1)

            dve.wait_ge(s_vlog, NT)
            dve.wait_ge(s_const, CONSTS)
            for t in range(NT):
                last = dve.max(top_v[:, t, :], logits[:, t, :])
            link(last)
            for t in range(NT):
                dve.match_replace(replaced[:, t, :], top_v[:, t, :], logits[:, t, :], TAKEN)
                last = dve.max_index(top_i[:, t, :], top_v[:, t, :], logits[:, t, :])
            link(last)
            dve.tensor_scalar(chosen[:, :, :], replaced[:, :, :], TAKEN, None, ALU.is_equal).then_inc(s_chosen, 1)
            dve.tensor_tensor(top_d[:, :, :], top_v[:, :, :], top_v[:, :, 0:1].to_broadcast([P, NT, K]),
                              ALU.subtract).then_inc(s_d, 1)
            dve.tensor_copy(rows[:, :, EXP:EXP + K], top_i[:, :, :])
            link(dve.tensor_copy(rows[:, :, TOK:TOK + 1], tok_i[:, :].rearrange("p (t a) -> p t a", a=1)))

            def count_and_map():
                dve.wait_ge(s_cnt, 1)
                link(dve.tensor_copy(cnt[:, :], ps[:, 3, 0:E]))
                link(dve.tensor_tensor_scan(end_e[:, :], ones[:, 0:E], cnt[:, :], 0.0, ALU.mult, ALU.add))
                link(dve.tensor_tensor(base_e[:, :], end_e[:, :], cnt[:, :], ALU.subtract))
                link(dve.scalar_tensor_tensor(slot_map[:, :, :], ps[:, 4, :].rearrange("p (t e) -> p t e", e=E), 1.0,
                                              base_e[:, :].rearrange("p (a e) -> p a e", a=1)
                                              .to_broadcast([P, NT, E]), ALU.add, ALU.add))
                dve.sem_inc(s_smap, 1)
                link(dve.tensor_tensor(slot_map[:, :, :], slot_map[:, :, :], chosen[:, :, :], ALU.mult))
                for t in range(NT):
                    last = dve.max(slot_f[:, t, :], slot_map[:, t, :])
                link(last)
                dve.tensor_scalar(slot_i[:, :, :], slot_f[:, :, :], -1.0, None, ALU.add).then_inc(s_sloti, 1)

            def weights():
                dve.wait_ge(s_e, 1)
                link(dve.tensor_reduce(top_s[:, :], top_e[:, :, :], AX.X, ALU.add))
                link(dve.reciprocal(top_r[:, :], top_s[:, :]))
                dve.scalar_tensor_tensor(rows[:, :, WGT:WGT + K], top_e[:, :, :], 0.5,
                                         top_r[:, :].rearrange("p (t a) -> p t a", a=1).to_broadcast([P, NT, K]),
                                         ALU.mult, ALU.mult).then_inc(s_route, 1)

            def tile_columns():
                link(dve.tensor_scalar(n_i[:, 0, :], cnt[:, :], float(P - 1), None, ALU.add))
                link(dve.tensor_scalar(n_i[:, 1, :], n_i[:, 0, :], P.bit_length() - 1, None, ALU.arith_shift_right))
                link(dve.tensor_scalar(n_e[:, :], n_i[:, 1, :], 1.0, None, ALU.max))
                link(dve.tensor_tensor_scan(t_end[:, :], ones[:, 0:E], n_e[:, :], 0.0, ALU.mult, ALU.add))
                dve.tensor_scalar(steps_f[:, :], t_end[:, E - 1:E], -2.0, None, ALU.add)
                link(dve.tensor_tensor(t_beg[:, :], t_end[:, :], n_e[:, :], ALU.subtract))
                dve.tensor_scalar(steps_i[:, :], steps_f[:, :], U.bit_length() - 1, None, ALU.arith_shift_right)
                dve.scalar_tensor_tensor(shift_e[:, :], t_beg[:, :], -float(P), base_e[:, :], ALU.mult, ALU.add)
                dve.tensor_scalar(is_le[:, 0, :], t_beg[:, :], part[:, 0:1], None, ALU.is_le)
                link(dve.tensor_scalar(is_le[:, 1, :], t_end[:, :], part[:, 0:1], None, ALU.is_le))
                dve.tensor_reduce(col[:, 0:1], is_le[:, 1, :], AX.X, ALU.add)
                link(dve.tensor_tensor(hot[:, :], is_le[:, 0, :], is_le[:, 1, :], ALU.subtract))
                dve.tensor_tensor_reduce(junk_e[:, 0, :], hot[:, :], shift_e[:, :], 1.0, 0.0, ALU.mult, ALU.add,
                                         col[:, 1:2])
                link(dve.tensor_tensor_reduce(junk_e[:, 1, :], hot[:, :], end_e[:, :], 1.0, 0.0, ALU.mult, ALU.add,
                                              col[:, 2:3]))
                dve.tensor_scalar(col[:, 3:4], col[:, 0:1], float(E - 1), None, ALU.min)
                link(dve.scalar_tensor_tensor(col[:, 4:5], part[:, 0:1], float(P), col[:, 1:2], ALU.mult, ALU.add))
                link(dve.tensor_scalar(col[:, 4:5], col[:, 4:5], float(PAIRS), None, ALU.min))
                link(dve.tensor_tensor(col[:, 5:6], col[:, 2:3], col[:, 4:5], ALU.subtract))
                for a, c in enumerate((4, 3, 5)):
                    last = dve.tensor_scalar(spread[:, a, :], ident[:, :], col[:, c:c + 1], None, ALU.mult)
                last.then_inc(s_spread, 1)

            def tables():
                link(dve.memset(tile_row[:, 0::2], PAIRS))
                dve.memset(tile_row[:, 1::2], 0)
                dve.memset(tile_exp[:, :], 0.0)
                link(dve.tensor_copy(tile_out[:, :], part[:, 1:2].to_broadcast([P, TILES])))
                dve.wait_ge(s_spread2, 1)
                dve.tensor_copy(tile_row[0:1, 0:2 * P:2], ps[0:1, 4, 0:P])
                dve.tensor_copy(tile_row[0:1, 1:2 * P:2], ps[0:1, 4, P:2 * P])
                dve.tensor_copy(tile_exp[:, 0:P], ps[:, 4, P:2 * P])
                dve.tensor_scalar(tile_out[:, 0:P], ps[:, 4, 2 * P:3 * P], part[:, 0:1], part[:, 1:2],
                                  ALU.is_le, ALU.mult).then_inc(s_table, 1)

            def use_max(g, i, j, u):
                unit = ("max", g, i, j, u)
                lo, width = a_units(i)[u]
                bank = a_bank(unit)[:, 0:width]
                dve.wait_ge(s_ap, a_no[unit] + 1)
                if lo + width == (i + 1) * P:
                    dve.tensor_tensor_reduce(bank, bank, mask_qk[:, HALF - width:HALF], 1.0, TAKEN, ALU.add, ALU.max,
                                             mx[:, g % 2, i // CT, j, i % CT:i % CT + 1]).then_inc(s_ad, 1)
                else:
                    dve.reduce_max(mx_low[:, g % 2, j, i % CT:i % CT + 1], bank, AX.X).then_inc(s_ad, 1)
                if (i, j, u) == (CT, HG - 1, len(a_units(i)) - 1):
                    dve.wait_ge(s_ad, a_no[unit] + 1)
                    dve.tensor_tensor(mx[:, g % 2, 1, :, :], mx[:, g % 2, 1, :, :], mx_low[:, g % 2, :, :],
                                      ALU.max).then_inc(s_mx, 1)

            def use_neg(g, c):
                unit = ("neg", g, c)
                dve.wait_ge(s_ap, a_no[unit] + 1)
                bank = a_bank(unit)[0:HG * CT, 0:P]
                link(dve.tensor_scalar(neg_hi[:, g % 2, c, :], bank, -1.0, None, ALU.mult))
                dve.scalar_tensor_tensor(neg_lo[:, g % 2, c, :], bank, -1.0, neg_hi[:, g % 2, c, :].bitcast(F32),
                                         ALU.mult, ALU.subtract).then_inc(s_neg, 1)
                dve.wait_ge(s_neg, 2 * g + 2 - c)
                dve.sem_inc(s_ad, 1)

            def use_post(g, q):
                unit = ("post", g, q)
                dve.wait_ge(s_ap, a_no[unit] + 1)
                bank = a_bank(unit).rearrange("p (t h c) -> p t h c", h=HG, c=VW)
                link(dve.reciprocal(rec[:, :, :].rearrange("p t (h a) -> p t h a", a=1), bank[:, :, :, DK:DK + 1]))
                dve.tensor_tensor(
                    att[:, 4 * q:4 * q + 4, g * HG * DK:(g + 1) * HG * DK].rearrange("p t (h c) -> p t h c", c=DK),
                    bank[:, :, :, 0:DK],
                    rec[:, :, :].rearrange("p t (h a) -> p t h a", a=1).to_broadcast([P, 4, HG, DK]),
                    ALU.mult).then_inc(s_att, 1)
                dve.wait_ge(s_att, 2 * g + q + 1)
                dve.sem_inc(s_ad, 1)

            use = {"max": use_max, "neg": use_neg, "post": use_post}
            for g in range(-1, G + 1):
                for step in range(NT):
                    for j in range(HG):
                        for kind, *what in a_at[(g, step, j)]:
                            use[kind](*what)
                    if g == -1 and step == 0:
                        count_and_map()
                    if g == 0 and step == 1:
                        weights()
                    if g == 1 and step == 1:
                        tile_columns()
            tables()

            for t in range(NT):
                dve.wait_ge(s_op, t + 1)
                dve.tensor_tensor(x_sb[:, t, :], ps[:, 2 + t % 2, 0:D], x_sb[:, t, :], ALU.add).then_inc(s_res, 1)

            dve.wait_ge(s_table, 1)
            more = dve.value_load(steps_i[0:1, 0:1], min_val=MIN_STEPS - 1, max_val=STEPS - 1)

            def meta(n, u, y, turn, added):
                dve.wait_ge(s_xg[u], 16 * turn + 16)
                wait_turn(dve, s_add[y], 16 * added)
                dve.scalar_tensor_tensor(w_junk[y][:, :], xg[u][:, EXP:EXP + K], tile_exp[:, bass.ds(n, 1)],
                                         xg[u][:, WGT:WGT + K], ALU.is_equal, ALU.mult, accum_out=w_slot[y][:, 0:1])
                dve.tensor_tensor(dst[y][:, 0:1], xg[u][:, TOK:TOK + 1], tile_out[:, bass.ds(n, 1)],
                                  ALU.max).then_inc(s_meta, 1)

            def rows_out(n, b):
                dve.wait_ge(s_T, n + 1)
                wait_turn(dve, s_gu, n - 1)
                dve.tensor_copy(xgT[b], ps[:, b, 0:DC * P]).then_inc(s_Te, 1)

            def hidden(n, b):
                dve.wait_ge(s_th, n + 1)
                dve.scalar_tensor_tensor(sg[b], th[b], 1.0, ps[0:I, 2 + b, 0:P],
                                         ALU.add, ALU.mult).then_inc(s_sg, 1)
                dve.wait_ge(s_sg, n + 1)
                wait_turn(dve, s_dn, n - 1)
                dve.tensor_tensor(hh[b], sg[b], ps[0:I, 2 + b, P:2 * P], ALU.mult).then_inc(s_h, 1)

            def step(s):
                for u in range(1, U + 1):
                    n = s * U + u
                    rows_out(n + 2, u % 2)
                    hidden(n, u % 2)
                    meta(n, u % U, u % NY, s + u // U, s * (U // NY) + u // NY)

            rows_out(0, 0)
            rows_out(1, 1)
            hidden(0, 0)
            meta(0, 0, 0, 0, 0)
            rows_out(2, 0)
            step(0)
            with dve.Fori(1, STEPS) as s:
                with dve.If(s <= more):
                    step(s)

            for j in range(NY):
                dve.wait_ge(s_yl[j], 16)
            a, b = slice(0, NT // 2), slice(NT // 2, NT)
            link(dve.tensor_tensor(sum_buf(0)[:, a], sum_buf(0)[:, a], sum_buf(1)[:, a], ALU.add))
            link(dve.tensor_tensor(sum_buf(0)[:, a], sum_buf(0)[:, a], sum_buf(2)[:, a], ALU.add))
            dve.tensor_tensor(sum_buf(0)[:, a], sum_buf(0)[:, a], sum_buf(3)[:, a], ALU.add).then_inc(s_fin[0], 1)
            link(dve.tensor_tensor(sum_buf(0)[:, b], sum_buf(0)[:, b], sum_buf(1)[:, b], ALU.add))
            dve.wait_ge(s_yp, 1)
            dve.tensor_tensor(sum_buf(0)[:, b], sum_buf(0)[:, b], sum_buf(2)[:, b], ALU.add).then_inc(s_fin[1], 1)


def kernel(**inputs):
    import numpy as np
    import concourse.bacc as bacc
    from concourse.bass_utils import run_bass_kernel_spmd

    f32 = np.float32
    inv = (f32(10000.0) ** (-(np.arange(0, DK, 2, dtype=f32) / f32(DK)))).astype(f32)
    ang = (np.arange(N, dtype=f32)[:, None] * inv).astype(f32)
    cos = np.repeat(np.cos(ang), 2, axis=1).astype(f32)
    sin = np.repeat(np.sin(ang), 2, axis=1).astype(f32) * np.tile(np.array([-1, 1], f32), DK // 2)

    def by_tile(a):
        return np.ascontiguousarray(a.reshape(NT, P, DK).transpose(1, 0, 2))

    a = {k: np.asarray(v) for k, v in inputs.items()}
    w_in = np.concatenate([a["L0_attn_wq"].T, a["L0_attn_wk"].T, a["L0_attn_wv"].T, a["L0_ffn_gate_weight"].T], 1)
    gu = np.concatenate([a["L0_ffn_w_gate"], a["L0_ffn_w_up"]], 2)
    gu = gu.reshape(E, DC, P, 2 * I).transpose(0, 2, 1, 3).reshape(E, P, DC * 2 * I)
    down = np.pad(a["L0_ffn_w_down"], ((0, 0), (0, P - I), (0, 0)))
    w_exp = np.concatenate([gu, down], 2)
    arrays = {
        "x": a["L0_attn_x"].reshape(N, D), "cos": by_tile(cos), "sin": by_tile(sin), "w_in": w_in,
        "w_out": a["L0_attn_wo"].T, "w_exp": w_exp,
    }
    arrays = {k: np.ascontiguousarray(v) for k, v in arrays.items()}
    nc = bacc.Bacc("TRN2", target_bir_lowering=False, num_devices=1)
    args = [nc.dram_tensor(k, v.shape, mybir.dt.from_np(v.dtype), kind="ExternalInput").ap() for k, v in arrays.items()]
    out = nc.dram_tensor("out", (N, D), F32, kind="ExternalOutput").ap()
    build(nc, *args, out)
    r = run_bass_kernel_spmd(nc, [arrays], core_ids=[0])
    return r.results[0]["out"].reshape(1, N, D)
```

```python
from contextlib import ExitStack

import concourse.bass as bass
from concourse import mybir

F32 = mybir.dt.float32
F32R = mybir.dt.float32r
BF16 = mybir.dt.bfloat16
I32 = mybir.dt.int32
U32 = mybir.dt.uint32
ALU = mybir.AluOpType
ACT = mybir.ActivationFunctionType
AX = mybir.AxisListType

P = 128
N = 1024
D = 256
NT = N // P
DC = D // P
H = 16
DK = D // H
HG = 4
G = H // HG
VW = 32
E = 64
K = 8
I = 96
ROW = D + 1 + 2 * K
TOK, EXP, WGT = D, D + 1, D + 1 + K
W_ROW = DC * 2 * I + D
MASKED = -1.0e30
TAKEN = -3.0e38
EPS = 1e-5
LN_BATCHES = (0, 2, 5, NT)
PAIRS = N * K
U = 8
FIRST = 2
STEPS = -(-(PAIRS // P + E - 1 - FIRST) // U)
MIN_STEPS = -(-(E - FIRST) // U)
TILES = STEPS * U + U
NY = 4
QUARTERS = 4
BOUNDED = "the tables are made with first slots clamped to PAIRS and experts to E - 1"
B_BANKS, PV_BANK, A_BANKS = (0, 1, 2), 3, (5, 6, 7)
HALF = N // 2
CT = NT // 2
AHEAD = HG * 12
FIRST_STEPS = 6
OUT_START = 12
NEG_LAG = 2
STAGE_DMAS = 5
SLOTS = 3


def a_units(i):
    width = (i + 1) * P
    return [(0, width)] if width <= 512 else [(0, 512), (512, width - 512)]


def halves(kt):
    return [(max(kt * P, lo), lo + HALF) for lo in (0, HALF) if kt * P < lo + HALF]


def attention_order():
    stream = []
    for g in range(G):
        tiles = list(reversed(range(NT)))
        if g == 0:
            tiles = tiles[CT:] + tiles[:CT]
        for n, i in enumerate(tiles):
            for j in range(HG):
                stream.append((i + 1, [("max", g, i, j, u) for u in range(len(a_units(i)))]))
                if j == NEG_LAG and n == CT:
                    stream.append((0, [("neg", g, tiles[0] // CT)]))
                if j == NEG_LAG and n == 0 and g > 1:
                    stream.append((0, [("neg", g - 1, 0)]))
        if g in (0, G - 1):
            stream.append((0, [("neg", g, tiles[-1] // CT)]))
    group_work = HG * NT * (NT + 1) // 2
    at, taken = {}, 0
    for g in range(-1, G + 1):
        weight = [step + 1 + (step or (NT if g > 0 else 0)) for step in range(NT)]
        for step in range(NT):
            for j in range(HG):
                here = at[(g, step, j)] = []
                if step == 1 and j == HG - 1 and g >= 1:
                    here += [("post", g - 1, q) for q in range(2)]
                if (g, step, j) == (1, 7, 3):
                    here.append(("table",))
                if g == G - 1 and step * HG + j >= OUT_START:
                    n = step * HG + j - OUT_START
                    here += [("att", n)] if n < NT else []
                    here += [("out", n - 1)] if 1 <= n <= NT else []
                if g < 0:
                    first = HG * CT * (CT + 1) // 2
                    share = first * (j + 1) // HG if step == 0 else \
                        first + (group_work + AHEAD - first) * min(step, FIRST_STEPS) // FIRST_STEPS
                else:
                    share = group_work * (g + 1) + AHEAD + group_work * (
                        sum(weight[:step]) * HG + weight[step] * (j + 1)) // (sum(weight) * HG)
                while stream and (taken < share or stream[0][0] == 0):
                    work, units = stream.pop(0)
                    taken += work
                    here += units
    return at


def wait_turn(eng, semaphore, value):
    if not isinstance(value, int) or value > 0:
        eng.wait_ge(semaphore, value)


def build(nc, x, cos, sin, w_in, w_out, w_gu, w_down, out):
    ctx = ExitStack()
    with ctx:
        def sb(name, shape, dt=F32):
            return ctx.enter_context(nc.sbuf_tensor(name, shape, dt))

        def sem(name):
            return ctx.enter_context(nc.semaphore(name))

        def dram(name, shape, dt=F32):
            return nc.dram_tensor(name, shape, dt).ap()

        WIN = 3 * D + E
        qk_parts = dram("qk_parts", [2 * D, 2, N])
        slots = dram("slots", [PAIRS + P, ROW])
        y_acc = [dram(f"y_acc{j}", [N + P, D]) for j in range(NY)]

        x_sb = sb("x_sb", [P, NT, D])
        rows = sb("rows", [P, NT, ROW])
        w_out_sb = sb("w_out_sb", [P, DC, D])
        ident = sb("ident", [P, P])
        ones = sb("ones", [P, P])
        ident_b = sb("ident_b", [P, P], BF16)
        ones_b = sb("ones_b", [P, P], BF16)
        zero_b = sb("zero_b", [P, P], BF16)
        before_b = sb("before_b", [P, P], BF16)
        mask_kq = sb("mask_kq", [P, P], BF16)
        mask_qk = sb("mask_qk", [P, 512], BF16)
        zero = sb("zero", [P, 3 * D])
        part = sb("part", [P, 2])
        stats = sb("stats", [P, NT, 6])
        moments = sb("moments", [P, NT, 2])
        rstd = sb("rstd", [P, NT])
        var_eps = sb("var_eps", [P, NT])
        minus_half = sb("minus_half", [P, NT])
        v_aug = sb("v_aug", [P, NT, H, VW])
        qz = [sb(f"qz{b}", [P, 2, HG, HALF], F32R) for b in range(SLOTS - 1)]
        kz = [sb(f"kz{b}", [P, 2, HG, HALF], F32R) for b in range(SLOTS - 1)]
        mx = sb("mx", [P, 2, 2, HG, CT])
        mx_low = sb("mx_low", [P, 2, HG, CT])
        neg_hi = sb("neg_hi", [HG * CT, 2, 2, P], F32R)
        neg_lo = sb("neg_lo", [HG * CT, 2, 2, P], F32R)
        probs = sb("probs", [P, 2, HG, N])
        att_raw = sb("att_raw", [P, N])
        rec = sb("rec", [P, 4, HG])
        att = sb("att", [P, NT, D])
        logits = sb("logits", [P, NT, E])
        top_v = sb("top_v", [P, NT, K])
        top_i = sb("top_i", [P, NT, K], U32)
        replaced = sb("replaced", [P, NT, E])
        chosen = sb("chosen", [P, NT, E], BF16)
        top_d = sb("top_d", [P, NT, K])
        top_e = sb("top_e", [P, NT, K])
        top_s = sb("top_s", [P, NT])
        top_r = sb("top_r", [P, NT])
        slot_map = replaced
        slot_f = sb("slot_f", [P, NT, K])
        slot_i = sb("slot_i", [P, NT, K], I32)
        tok_i = sb("tok_i", [P, NT], I32)
        cnt = sb("cnt", [P, E])
        end_e = sb("end_e", [P, E])
        base_e = sb("base_e", [P, E])
        n_i = sb("n_i", [P, 2, E], I32)
        n_e = sb("n_e", [P, E])
        t_end = sb("t_end", [P, E])
        t_beg = sb("t_beg", [P, E])
        shift_e = sb("shift_e", [P, E])
        is_le = sb("is_le", [P, 2, E])
        hot = sb("hot", [P, E])
        junk_e = sb("junk_e", [P, 2, E])
        col = sb("col", [P, 6])
        spread = sb("spread", [P, 3, P])
        tile_e = sb("tile_e", [1, TILES], I32)
        tile_row = sb("tile_row", [1, 2 * TILES], I32)
        tile_exp = sb("tile_exp", [P, TILES])
        tile_out = sb("tile_out", [P, TILES])
        steps_f = sb("steps_f", [P, 1], I32)
        steps_i = sb("steps_i", [P, 1], I32)
        def part_of(flat, n, width, rows_=P):
            return flat[0:rows_, n * width:(n + 1) * width]

        v_flat = v_aug[:, :, :, :].rearrange("p t h c -> p (t h c)")
        probs_flat = probs[:, :, :, :].rearrange("p b h n -> p (b h n)")
        att_flat = att[:, :, :].rearrange("p t d -> p (t d)")
        attT = probs_flat[:, U * W_ROW:U * W_ROW + N]
        attT_first = rows[:, :, :].rearrange("p t r -> p (t r)")[:, 0:N]
        xg = [part_of(v_flat[:, NT * H * VW - U * ROW:NT * H * VW], u, ROW) for u in range(U)]
        w_all = [part_of(probs_flat, u, W_ROW) for u in range(U)]
        wgu = [w[:, 0:DC * 2 * I] for w in w_all]
        wdn = [w[0:I, DC * 2 * I:W_ROW] for w in w_all]
        y_sb = [part_of(att_raw, u, D) for u in range(NY)]
        xgT = [part_of(att_flat, u, D) for u in range(2)]
        th = [part_of(att_flat, 4 + u, P, I) for u in range(2)]
        sg = [part_of(att_flat, 6 + u, P, I) for u in range(2)]
        hidden_sb = sb("hidden_sb", [I, 2 * P])
        hh = [hidden_sb[:, u * P:(u + 1) * P] for u in range(2)]
        w_junk = [sb(f"w_junk{u}", [P, K]) for u in range(NY)]
        w_slot = [sb(f"w_slot{u}", [P, 1]) for u in range(NY)]
        dst = [sb(f"dst{u}", [P, 1], I32) for u in range(NY)]

        front = ExitStack()

        def front_sb(name, shape, dt=F32):
            return front.enter_context(nc.sbuf_tensor(name, shape, dt))

        cos_sb = front_sb("cos_sb", [P, NT, DK])
        sin_sb = front_sb("sin_sb", [P, NT, DK])
        w_in_sb = front_sb("w_in_sb", [P, DC, WIN])
        xnT = front_sb("xnT", [P, DC, N])
        rope_c = front_sb("rope_c", [P, 2, 2 * D])
        rope_s = front_sb("rope_s", [P, 2, 2 * D])
        qk_rot = front_sb("qk_rot", [P, 2, 2 * D])
        part_hi = front_sb("part_hi", [P, 2, 4 * P], F32R)
        part_lo = front_sb("part_lo", [P, 2, 4 * P], F32R)
        front.close()
        qz.append(sb("qz2", [P, 2, HG, HALF], F32R))
        kz.append(sb("kz2", [P, 2, HG, HALF], F32R))

        ps = ctx.enter_context(nc.psum_tensor("ps", [P, 8, 512], F32))

        s_x = [sem(f"x_loaded{t}") for t in range(NT)]
        s_wqk = sem("qk_weights_loaded")
        s_w = sem("weights_loaded")
        s_rope_tab = sem("rope_tables_loaded")
        s_const = sem("constants_ready")
        s_pchain = sem("pool_chain")
        s_vchain = sem("vector_chain")
        s_zero = sem("zeros_ready")
        s_clear = [sem(f"spare_rows_set{b}") for b in range(SLOTS)]
        s_zeroed = sem("scratch_zeroed")
        s_var = sem("variances_ready")
        s_rstd = sem("rstd_ready")
        s_ident = sem("identity_ready")
        s_xn = sem("rows_normalised")
        s_xT = sem("rows_transposed")
        s_xTe = sem("xnT_ready")
        s_proj = sem("qk_projected")
        s_projv = sem("v_projected")
        s_vlog = sem("v_and_logits_out")
        s_rope = sem("rope_products")
        s_rot = sem("qk_rotated")
        s_qkT = sem("qk_transposed")
        s_hi = sem("hi_ready")
        s_lo = sem("lo_ready")
        s_parts = [sem(f"parts_stored{b}") for b in range(2)]
        s_staged = [[sem(f"heads_staged{b}{c}") for c in range(2)] for b in range(SLOTS)]
        s_ap = sem("a_unit_made")
        s_ad = sem("a_unit_used")
        s_mx = sem("maxima_ready")
        s_neg = sem("negmax_ready")
        s_negd = [[sem(f"negmax_placed{b}{c}") for c in range(2)] for b in range(SLOTS)]
        s_bp = sem("scores_made")
        s_be = sem("probs_ready")
        s_pv = sem("pv_done")
        s_acc = sem("att_out")
        s_att = sem("att_normalised")
        s_aT = sem("att_transposed")
        s_aTe = sem("attT_ready")
        s_op = sem("out_projected")
        s_res = sem("residual_ready")
        s_resd = sem("residual_stored")
        s_chosen = sem("chosen_ready")
        s_d = sem("top_differences")
        s_e = sem("top_exponentials")
        s_route = sem("rows_complete")
        s_cnt = sem("counts_made")
        s_smap = sem("counts_used")
        s_sloti = sem("slot_numbers")
        s_scat = sem("rows_scattered")
        s_spread = sem("tile_columns")
        s_table = sem("tile_tables")
        s_xg = [sem(f"tile_rows{u}") for u in range(U)]
        s_wt = [sem(f"tile_gate_up_loaded{u}") for u in range(U)]
        s_wd = [sem(f"tile_down_loaded{u}") for u in range(U)]
        s_T = sem("tile_transposed")
        s_Te = sem("tile_xT_ready")
        s_gu = sem("tile_gate_up")
        s_th = sem("tile_tanh")
        s_sg = sem("tile_silu")
        s_h = sem("tile_hidden")
        s_dn = sem("tile_down")
        s_meta = sem("tile_destinations")
        s_y = sem("tile_result")
        s_add = [sem(f"tile_added{u}") for u in range(NY)]
        s_yl = [sem(f"results_loaded{k}") for k in range(NY - 1)]
        s_yq = [sem(f"last_results_loaded{q}") for q in range(QUARTERS)]
        s_turn = sem("tile_may_be_added")
        s_fin = sem("buffer_summed")
        s_out = sem("stored")

        CONSTS = 9

        a_at = attention_order()
        a_order = [unit for units in a_at.values() for unit in units]
        a_no = {unit: n for n, unit in enumerate(a_order)}
        neg_order = [unit[1:] for unit in a_order if unit[0] == "neg"]

        def a_bank(unit):
            return ps[:, A_BANKS[a_no[unit] % len(A_BANKS)], :]

        b_order = [(g, kt, j, lo) for g in range(G) for kt in reversed(range(NT)) for j in range(HG)
                   for lo, _ in halves(kt)]
        b_numbers = {unit: n for n, unit in enumerate(b_order)}

        def b_no(g, kt, j, lo=None):
            return b_numbers[(g, kt, j, halves(kt)[-1][0] if lo is None else lo)]

        def head_rows(tile, g, j, tile_no, rows_):
            c, t = divmod(tile_no, CT)
            return tile[g % SLOTS][0:rows_, c, j, t * P:(t + 1) * P]

        def sum_buf(k):
            j = NY - 1 - k
            return probs[:, j // 2, 2 * (j % 2):2 * (j % 2) + 2, :].rearrange("p a (t d) -> p (a t) d", d=D)

        def additions(more, j):
            return more * (16 * U // NY) + 16 * (U // NY + (j < FIRST))

        def quarter(q):
            return slice(q * NT // QUARTERS, (q + 1) * NT // QUARTERS)

        block = ctx.enter_context(nc.Block())

        @block.sync
        def _(sp):
            xv = x.rearrange("(t p) d -> t p d", p=P)
            w_in_rows = w_in.rearrange("(c p) n -> p c n", p=P)
            for t in range(NT):
                sp.dma_start(x_sb[:, t, :], xv[t]).then_inc(s_x[t], 16)
                if t == 1:
                    sp.dma_start(w_in_sb[:, :, 0:2 * D], w_in_rows[:, :, 0:2 * D]).then_inc(s_wqk, 16)
            sp.dma_start(w_in_sb[:, :, 2 * D:WIN], w_in_rows[:, :, 2 * D:WIN]).then_inc(s_w, 16)
            sp.dma_start(w_out_sb[:, :, :], w_out.rearrange("(c p) n -> p c n", p=P)).then_inc(s_w, 16)
            def clear_rows(b):
                sp.wait_ge(s_zero, 2)
                for tile, lo, hi, src in ((qz, 64, P, zero), (kz, 64, 96, zero), (kz, 96, 98, ones), (kz, 98, P, zero)):
                    sp.dma_start(tile[b][lo:hi].bitcast(F32).rearrange("p c h (a n) -> p (c h a) n", n=P),
                                 src[lo:hi, 0:P].rearrange("p (a n) -> p a n", a=1)
                                 .to_broadcast([hi - lo, HG * NT, P])).then_inc(s_clear[b], 16)

            def zero_scratch():
                for j in range(NY):
                    for r in range(0, N + P, 3 * P):
                        sp.dma_start(y_acc[j][r:r + 3 * P, :].rearrange("(p a) d -> p (a d)", a=3),
                                     zero[:, :]).then_inc(s_zeroed, 16)
                sp.dma_start(slots[PAIRS:PAIRS + P, :], zero[:, 0:ROW]).then_inc(s_zeroed, 16)

            def store_parts(t):
                for w, (tile, ready) in enumerate(((part_hi, s_hi), (part_lo, s_lo))):
                    sp.wait_ge(ready, t + 1)
                    sp.dma_start(qk_parts[:, w, :].rearrange("(b p) n -> p b n", p=P)[:, :, t * P:(t + 1) * P],
                                 tile[:, t % 2, :].bitcast(F32).rearrange("p (b n) -> p b n", n=P),
                                 ).then_inc(s_parts[t % 2], 16)

            def stage_k(g, c):
                f, n = D + g * HG * DK, slice(c * HALF, (c + 1) * HALF)
                parts = qk_parts[f:f + HG * DK, :, n]
                for r, step, src in ((0, 1, parts), (32, 2, parts[:, 1:2]), (33, 2, parts[:, 0:1])):
                    sp.dma_start(kz[g % SLOTS][r:r // 32 * 32 + 32:step, c, :, :].bitcast(F32),
                                 src.rearrange("(j f) w n -> (f w) j n", j=HG)).then_inc(s_staged[g % SLOTS][c], 16)

            def stage_q(g, c):
                f, n = g * HG * DK, slice(c * HALF, (c + 1) * HALF)
                for r in (0, 32):
                    sp.dma_start(qz[g % SLOTS][r:r + 2 * DK, c, :, :].bitcast(F32),
                                 qk_parts[f:f + HG * DK, :, n].rearrange("(j f) w n -> (f w) j n", j=HG),
                                 ).then_inc(s_staged[g % SLOTS][c], 16)

            def stage(g, c):
                stage_k(g, c)
                stage_q(g, c)

            def place_negmax(g, c):
                sp.wait_ge(s_neg, neg_order.index((g, c)) + 1)
                sp.wait_ge(s_clear[g % SLOTS], 16 * 4)
                for r, src in ((96, neg_hi), (97, neg_lo)):
                    sp.dma_start(qz[g % SLOTS][r:r + 1, c, :, :].bitcast(F32).rearrange("o h (i q) -> o (h i) q", q=P),
                                 src[:, g % 2, c, :].bitcast(F32)).then_inc(s_negd[g % SLOTS][c], 16)

            sp.wait_ge(s_w, 32)
            clear_rows(0)
            for t in range(NT):
                store_parts(t)
                if t == CT:
                    for b in range(2):
                        sp.wait_ge(s_parts[b], 16 * CT)
                    stage(0, 0)
            for b in range(2):
                sp.wait_ge(s_parts[b], 16 * NT)
            stage(0, 1)
            stage(1, 1)
            stage(1, 0)
            clear_rows(1)
            place_negmax(0, 0)
            sp.wait_ge(s_vlog, NT)
            clear_rows(2)
            stage(2, 1)
            stage(2, 0)
            place_negmax(0, 1)
            zero_scratch()
            for g, c in neg_order[2:]:
                if (g, c) == (2, 1):
                    sp.wait_ge(s_bp, b_no(0, 0, HG - 1) + 1)
                    stage(3, 1)
                    stage(3, 0)
                place_negmax(g, c)

            sp.wait_ge(s_table, 1)
            sp.wait_ge(s_scat, 16 * NT * K)
            more = sp.value_load(steps_i[0:1, 0:1], min_val=MIN_STEPS - 1, max_val=STEPS - 1)

            def numbers(turn):
                _, v = nc.values_load_multi_w_load_instructions(
                    tile_row[0:1, bass.ds(turn * (2 * U), 2 * U)], engines=[mybir.EngineType.SP],
                    min_val=0, max_val=PAIRS, skip_runtime_bounds_check_because=BOUNDED)
                return [(v[2 * u], nc.s_assert_within(v[2 * u + 1], 0, E - 1,
                                                      skip_runtime_bounds_check_because=BOUNDED)) for u in range(U)]

            def load_rows(first, u):
                sp.dma_start(xg[u], slots[bass.ds(first, P), :]).then_inc(s_xg[u], 16)

            def load_weights(expert, u):
                sp.dma_start(wgu[u], w_gu[bass.ds(expert, 1), :, :].rearrange("a p i -> (a p) i")).then_inc(s_wt[u], 16)

            first_tiles = numbers(0)
            done = -(-U * ROW // (H * VW))
            sp.wait_ge(s_pv, (G - 1) * NT + done)
            for u, (first, _) in enumerate(first_tiles):
                load_rows(first, u)
            for u, (_, expert) in enumerate(first_tiles):
                if u == 0:
                    sp.wait_ge(s_pv, G * NT - 1)
                if u == HG * N // W_ROW:
                    sp.wait_ge(s_pv, G * NT)
                load_weights(expert, u)
                sp.dma_start(wdn[u], w_down[bass.ds(expert, 1), :, :].rearrange("a i d -> (a i) d")).then_inc(s_wd[u], 16)
            sp.wait_ge(s_zeroed, 16 * (3 * NY + 1))
            sp.wait_ge(s_res, NT // 2)
            sp.dma_start(y_acc[0][0:N, :].rearrange("(t p) d -> p t d", p=P), x_sb[:, :, :]).then_inc(s_resd, 16)

            with sp.Fori(0, STEPS) as s:
                with sp.If(s <= more):
                    for u, (first, expert) in enumerate(numbers(s + 1)):
                        last = s * U + u
                        sp.wait_ge(s_T, last + 1)
                        sp.wait_ge(s_meta, last + 1)
                        load_rows(first, u)
                        sp.wait_ge(s_gu, last + 1)
                        load_weights(expert, u)

            for u in range(U):
                sp.wait_ge(s_xg[u], more * 16 + 32)
                sp.wait_ge(s_wt[u], more * 16 + 32)
                sp.wait_ge(s_wd[u], more * 16 + 32)
            yv = [y_acc[j][0:N, :].rearrange("(t p) d -> p t d", p=P) for j in range(NY)]
            for k in range(NY):
                j = (FIRST + k) % NY
                sp.wait_ge(s_add[j], additions(more, j))
                if k < NY - 1:
                    sp.dma_start(sum_buf(k), yv[j]).then_inc(s_yl[k], 16)
                if k == 0:
                    sp.wait_ge(s_dn, more * U + U + FIRST)
            for q in range(QUARTERS):
                sp.dma_start(sum_buf(NY - 1)[:, quarter(q), :], yv[j][:, quarter(q), :]).then_inc(s_yq[q], 16)
            for q in range(QUARTERS):
                sp.wait_ge(s_fin, q + 1)
                sp.dma_start(out.rearrange("(t p) d -> p t d", p=P)[:, quarter(q), :],
                             sum_buf(0)[:, quarter(q), :]).then_inc(s_out, 16)
            sp.wait_ge(s_resd, 16)
            sp.wait_ge(s_out, 16 * QUARTERS)

        @block.gpsimd
        def _(pool):
            chained = [0]

            def link(ins):
                chained[0] += 1
                ins.then_inc(s_pchain, 1)
                pool.wait_ge(s_pchain, chained[0])

            link(pool.memset(ident[:, :], 0.0))
            pool.affine_select(out=ident[:, :], in_=ident[:, :], compare_op=ALU.not_equal, fill=1.0, base=0,
                               pattern=[[-1, P]], channel_multiplier=1).then_inc(s_ident, 1)
            pool.memset(zero[:, :], 0.0).then_inc(s_zero, 1)
            pool.memset(ones[:, :], 1.0).then_inc(s_zero, 1)
            link(pool.memset(minus_half[:, :], -0.5))
            for lo, hi in zip(LN_BATCHES, LN_BATCHES[1:]):
                pool.wait_ge(s_var, hi)
                pool.tensor_tensor(rstd[:, lo:hi], var_eps[:, lo:hi], minus_half[:, lo:hi], ALU.pow).then_inc(s_rstd, 1)
            def constants(n):
                if n == 0:
                    link(pool.memset(ident_b[:, :], 0.0))
                    pool.affine_select(out=ident_b[:, :], in_=ident_b[:, :], compare_op=ALU.not_equal, fill=1.0, base=0,
                                       pattern=[[-1, P]], channel_multiplier=1).then_inc(s_const, 1)
                    pool.memset(ones_b[:, :], 1.0).then_inc(s_const, 1)
                    pool.memset(zero_b[:, :], 0.0).then_inc(s_const, 1)
                if n == 1:
                    link(pool.memset(before_b[:, :], 1.0))
                    pool.affine_select(out=before_b[:, :], in_=before_b[:, :], compare_op=ALU.is_gt, fill=0.0, base=0,
                                       pattern=[[1, P]], channel_multiplier=-1).then_inc(s_const, 1)
                if n == 2:
                    link(pool.memset(mask_kq[:, :], 0.0))
                    pool.affine_select(out=mask_kq[:, :], in_=mask_kq[:, :], compare_op=ALU.is_ge, fill=MASKED, base=0,
                                       pattern=[[1, P]], channel_multiplier=-1).then_inc(s_const, 1)
                if n == 3:
                    link(pool.memset(mask_qk[:, :], 0.0))
                    pool.affine_select(out=mask_qk[:, :], in_=mask_qk[:, :], compare_op=ALU.is_ge, fill=MASKED,
                                       base=HALF - P, pattern=[[-1, HALF]], channel_multiplier=1).then_inc(s_const, 1)
                if n == 4:
                    pool.iota(tok_i[:, :], [[P, NT]], base=0, channel_multiplier=1).then_inc(s_const, 1)
                    pool.iota(part[:, :], [[N, 2]], base=0, channel_multiplier=1,
                              allow_small_or_imprecise_dtypes=True).then_inc(s_const, 1)
                if n == 5:
                    link(pool.memset(v_aug[:, :, :, DK:VW], 0.0))
                    pool.memset(v_aug[:, :, :, DK:DK + 1], 1.0).then_inc(s_const, 1)

            for t in range(NT):
                pool.wait_ge(s_rope, 3 * (t + 1))
                if t >= 2:
                    pool.wait_ge(s_qkT, t - 1)
                pool.tensor_tensor(qk_rot[:, t % 2, :], rope_c[:, t % 2, :], rope_s[:, t % 2, :],
                                   ALU.add).then_inc(s_rot, 1)
                constants(t)

            pool.wait_ge(s_route, 1)
            pool.wait_ge(s_sloti, 1)
            for t in range(NT):
                for k in range(K):
                    pool.indirect_dma_start(slots[:, :], bass.IndirectOffsetOnAxis(ap=slot_i[:, t, k:k + 1], axis=0),
                                            rows[:, t, :], None).then_inc(s_scat, 16)

            pool.wait_ge(s_resd, 16)
            pool.wait_ge(s_zeroed, 16 * (3 * NY + 1))

            def add(n, u, before):
                pool.wait_ge(s_y, n + 1)
                wait_turn(pool, s_add[u], 16 * before)
                pool.sem_inc(s_turn, 1)
                pool.indirect_dma_start(y_acc[u][:, :], bass.IndirectOffsetOnAxis(ap=dst[u][:, 0:1], axis=0),
                                        y_sb[u], None, compute_op=ALU.add).then_inc(s_add[u], 16)

            more = pool.value_load(steps_i[0:1, 0:1], min_val=MIN_STEPS - 1, max_val=STEPS - 1)

            def step(s):
                for u in range(FIRST, U + FIRST):
                    add(s * U + u, u % NY, s * (U // NY) + u // NY)

            for n in range(FIRST):
                add(n, n, 0)
            step(0)
            with pool.Fori(1, STEPS) as s:
                with pool.If(s <= more):
                    step(s)

        @block.scalar
        def _(act):
            act.dma_start(cos_sb[:, :, :], cos).then_inc(s_rope_tab, 16)
            act.dma_start(sin_sb[:, :, :], sin).then_inc(s_rope_tab, 16)

            def xT_out(t):
                act.wait_ge(s_xT, t + 1)
                act.activation(xnT[:, :, t * P:(t + 1) * P],
                               ps[:, t % 2, 0:DC * P].rearrange("p (c n) -> p c n", n=P), ACT.Copy).then_inc(s_xTe, 1)

            def v_out(t):
                act.wait_ge(s_projv, t + 1)
                act.activation(v_aug[:, t, :, 0:DK], ps[:, t % 2, 0:D].rearrange("p (h c) -> p h c", c=DK), ACT.Copy)
                act.activation(logits[:, t, :], ps[:, t % 2, D:D + E], ACT.Copy).then_inc(s_vlog, 1)

            def hi_out(t):
                act.wait_ge(s_qkT, t + 1)
                if t >= 2:
                    act.wait_ge(s_parts[t % 2], 32 * (t // 2))
                act.activation(part_hi[:, t % 2, :], ps[:, 6 + t % 2, :], ACT.Copy).then_inc(s_hi, 1)

            xT_out(0)
            for t in range(NT):
                if t + 1 < NT:
                    xT_out(t + 1)
                if t >= 1:
                    hi_out(t - 1)
            v_out(0)
            v_out(1)
            hi_out(NT - 1)
            for t in range(2, NT):
                v_out(t)

            def exps(g, step, j):
                kt = NT - 1 - step
                if step >= 2 or g > 0:
                    act.wait_ge(s_pv, g * NT + step - 1)
                for lo, hi in halves(kt):
                    n = b_no(g, kt, j, lo)
                    act.wait_ge(s_bp, n + 1)
                    act.activation(probs[:, step % 2, j, lo:hi],
                                   ps[:, B_BANKS[n % len(B_BANKS)], lo % HALF:(hi - 1) % HALF + 1],
                                   ACT.Exp, scale=DK ** -0.5).then_inc(s_be, 1)

            def att_out(g):
                act.wait_ge(s_pv, (g + 1) * NT)
                if g >= 1:
                    act.wait_ge(s_ap, a_no[("post", g - 1, 1)] + 1)
                act.activation(att_raw[:, :], ps[:, PV_BANK:PV_BANK + 2, :].rearrange("p a b -> p (a b)"),
                               ACT.Copy).then_inc(s_acc, 1)

            for g in range(G):
                for step in range(NT):
                    for j in range(HG):
                        exps(g, step, j)
                    if g == 0 and step == 0:
                        act.wait_ge(s_d, 1)
                        act.activation(top_e[:, :, :], top_d[:, :, :], ACT.Exp).then_inc(s_e, 1)
                    if g > 0 and step == 0:
                        att_out(g - 1)
            att_out(G - 1)
            act.wait_ge(s_table, 1)
            more = act.value_load(steps_i[0:1, 0:1], min_val=MIN_STEPS - 1, max_val=STEPS - 1)
            def experts(turn):
                return nc.values_load_multi_w_load_instructions(
                    tile_e[0:1, bass.ds(turn * U, U)], engines=[mybir.EngineType.Activation],
                    min_val=0, max_val=E - 1, skip_runtime_bounds_check_because=BOUNDED)[1]

            def load_down(expert, u):
                act.dma_start(wdn[u], w_down[bass.ds(expert, 1), :, :].rearrange("a i d -> (a i) d")).then_inc(s_wd[u], 16)

            for q in range(2):
                act.wait_ge(s_aT, q + 1)
                act.activation(attT[:, q * HALF:(q + 1) * HALF], ps[:, q, :], ACT.Copy).then_inc(s_aTe, 1)


            def tanh(n, b):
                act.wait_ge(s_gu, n + 1)
                wait_turn(act, s_h, n - 1)
                act.activation(th[b], ps[0:I, 2 + b, 0:P], ACT.Tanh, scale=0.5).then_inc(s_th, 1)

            def result(n, u, b, added):
                act.wait_ge(s_dn, n + 1)
                act.wait_ge(s_meta, n + 1)
                wait_turn(act, s_add[u], 16 * added)
                act.activation(y_sb[u], ps[:, 4 + b, 0:D], ACT.Copy, scale=w_slot[u][:, 0:1]).then_inc(s_y, 1)

            def step(s):
                later = experts(s + 1)
                for u in range(FIRST, U + FIRST):
                    n = s * U + u
                    tanh(n, u % 2)
                    result(n - 1, (u - 1) % NY, (u - 1) % 2, s * (U // NY) + (u - 1) // NY)
                    load_down(later[u - FIRST], u - FIRST)

            tanh(0, 0)
            for n in range(1, FIRST):
                tanh(n, n)
                result(n - 1, n - 1, n - 1, 0)
            step(0)
            with act.Fori(1, STEPS) as s:
                with act.If(s <= more):
                    step(s)
            result(more * U + U + FIRST - 1, FIRST - 1, FIRST - 1, more * (U // NY) + U // NY)

        @block.tensor
        def _(pe):
            def x_transpose(t):
                pe.wait_ge(s_xn, t + 1)
                if t >= 2:
                    pe.wait_ge(s_xTe, t - 1)
                for c in range(DC):
                    last = pe.transpose(ps[:, t % 2, c * P:(c + 1) * P], rows[:, t, c * P:(c + 1) * P], ident[:, :])
                last.then_inc(s_xT, 1)

            def project(t):
                pe.wait_ge(s_xTe, t + 1)
                if t >= 2:
                    pe.wait_ge(s_rope, 3 * (t - 1))
                for c in range(DC):
                    last = pe.matmul(ps[:, 2 + t % 2, 0:2 * D], xnT[:, c, t * P:(t + 1) * P],
                                     w_in_sb[:, c, 0:2 * D], start=(c == 0), stop=(c == DC - 1))
                last.then_inc(s_proj, 1)

            def project_v(t):
                if t >= 2:
                    pe.wait_ge(s_vlog, t - 1)
                else:
                    pe.wait_ge(s_xTe, NT)
                for c in range(DC):
                    last = pe.matmul(ps[:, t % 2, 0:WIN - 2 * D], xnT[:, c, t * P:(t + 1) * P],
                                     w_in_sb[:, c, 2 * D:WIN], start=(c == 0), stop=(c == DC - 1))
                last.then_inc(s_projv, 1)

            def qk_transpose(t):
                pe.wait_ge(s_rot, t + 1)
                if t >= 2:
                    pe.wait_ge(s_lo, t - 1)
                for b in range(4):
                    last = pe.transpose(ps[:, 6 + t % 2, b * P:(b + 1) * P], qk_rot[:, t % 2, b * P:(b + 1) * P],
                                        ident[:, :])
                last.then_inc(s_qkT, 1)

            pe.wait_ge(s_ident, 1)
            x_transpose(0)
            pe.wait_ge(s_wqk, 16)
            for t in range(NT):
                if t + 1 < NT:
                    x_transpose(t + 1)
                project(t)
                if t >= 1:
                    qk_transpose(t - 1)
            pe.wait_ge(s_w, 32)
            project_v(0)
            project_v(1)
            qk_transpose(NT - 1)

            pe.wait_ge(s_const, CONSTS)
            pe.wait_ge(s_lo, NT)

            def counts():
                pe.wait_ge(s_chosen, 1)
                for t in range(NT):
                    pe.matmul(ps[:, 3, 0:E], ones_b[:, :], chosen[:, t, :], start=(t == 0), stop=(t == NT - 1))
                for t in range(NT):
                    for s in range(t + 1):
                        last = pe.matmul(ps[:, 4, t * E:(t + 1) * E], before_b[:, :] if s == t else ones_b[:, :],
                                         chosen[:, s, :], start=(s == 0), stop=(s == t))
                last.then_inc(s_cnt, 1)

            def a_free(unit):
                n = a_no[unit]
                if n >= len(A_BANKS):
                    pe.wait_ge(s_ad, n - len(A_BANKS) + 1)
                return a_bank(unit)

            def max_scores(g, i, j, u):
                lo, width = a_units(i)[u]
                if (j, u) == (0, 0):
                    for c in range(1 if g == 0 and i < CT else 2):
                        pe.wait_ge(s_staged[g % SLOTS][c], 16 * STAGE_DMAS * (g // SLOTS + 1))
                    pe.wait_ge(s_clear[g % SLOTS], 16 * 4)
                bank = a_free(("max", g, i, j, u))
                pe.matmul(bank[:, 0:width], head_rows(qz, g, j, i, 96), kz[g % SLOTS][0:96, lo // HALF, j, 0:width],
                          start=True, stop=True).then_inc(s_ap, 1)

            def neg_transpose(g, c):
                bank = a_free(("neg", g, c))
                if c == 1:
                    pe.wait_ge(s_mx, g + 1)
                else:
                    pe.wait_ge(s_ad, a_no[("max", g, 0, HG - 1, 0)] + 1)
                pe.transpose(bank[0:HG * CT, 0:P], mx[:, g % 2, c, :, :].rearrange("p h i -> p (h i)"),
                             ident[:, :]).then_inc(s_ap, 1)

            def scores(g, kt, j):
                for lo, hi in halves(kt):
                    n = b_no(g, kt, j, lo)
                    if n >= len(B_BANKS):
                        pe.wait_ge(s_be, n - len(B_BANKS) + 1)
                    a, b = lo % HALF, (hi - 1) % HALF + 1
                    bank = ps[:, B_BANKS[n % len(B_BANKS)], :]
                    last = pe.matmul(bank[:, a:b], head_rows(kz, g, j, kt, P), qz[g % SLOTS][:, lo // HALF, j, a:b],
                                     start=True, stop=True, skip_group_check=True)
                    if lo == kt * P:
                        last = pe.matmul(bank[:, a:a + P], ident_b[:, :], mask_kq[:, :], start=False, stop=True,
                                         skip_group_check=True)
                    last.then_inc(s_bp, 1)

            def pv(g, step, half):
                kt = NT - 1 - step
                if half == 0:
                    pe.wait_ge(s_be, b_no(g, kt, HG - 1) + 1)
                    if step == 0:
                        if g >= 1:
                            pe.wait_ge(s_acc, g)
                        for b in range(2):
                            pe.matmul(ps[:, PV_BANK + b, :], zero_b[:, :], mask_qk[:, :], start=True, stop=True)
                ranges = halves(kt)
                last = None
                if half == 0 or len(ranges) == 2:
                    lo, hi = ranges[-1 - half]
                    for j in range(HG):
                        last = pe.matmul(ps[VW * j:VW * (j + 1), PV_BANK + lo // HALF, lo % HALF:(hi - 1) % HALF + 1],
                                         v_aug[:, kt, g * HG + j, :], probs[:, step % 2, j, lo:hi],
                                         start=False, stop=True, skip_group_check=True)
                if half == len(ranges) - 1:
                    last.then_inc(s_pv, 1)

            def post(g, q):
                bank = a_free(("post", g, q))
                pe.wait_ge(s_acc, g + 1)
                for t in range(4):
                    last = pe.transpose(bank[:, t * P:(t + 1) * P], att_raw[:, (4 * q + t) * P:(4 * q + t + 1) * P],
                                        ident[:, :])
                last.then_inc(s_ap, 1)

            def spread_columns():
                bank = a_free(("table",))
                pe.wait_ge(s_spread, 1)
                pe.matmul(bank[:, 0:3 * P], ones[:, :], spread[:, :, :].rearrange("p a b -> p (a b)"),
                          start=True, stop=True).then_inc(s_ap, 1)

            def att_transpose(t):
                bank = a_free(("att", t))
                pe.wait_ge(s_att, 4)
                pe.transpose(bank[:, 0:P], att[:, t, 0:P], ident[:, :]).then_inc(s_ap, 1)

            def out_first(t):
                bank = a_free(("out", t))
                pe.wait_ge(s_ad, a_no[("att", t)] + 1)
                pe.matmul(bank[:, 0:D], attT_first[:, t * P:(t + 1) * P], w_out_sb[:, 0, :],
                          start=True, stop=True).then_inc(s_ap, 1)

            make = {"max": max_scores, "neg": neg_transpose, "post": post, "table": spread_columns,
                    "att": att_transpose, "out": out_first}
            for g in range(-1, G + 1):
                for step in range(NT):
                    kt = NT - 1 - step
                    if step == 0 and 0 <= g < G:
                        pe.wait_ge(s_negd[g % SLOTS][1], 32 * (g // SLOTS + 1))
                    if kt == CT - 1 and 0 <= g < G:
                        pe.wait_ge(s_negd[g % SLOTS][0], 32 * (g // SLOTS + 1))
                    if step == 0 and g == 0:
                        pe.wait_ge(s_smap, 1)
                    for j in range(HG):
                        if 0 <= g < G:
                            scores(g, kt, j)
                        for kind, *what in a_at[(g, step, j)]:
                            make[kind](*what)
                        if j % 2 == 1 and 0 <= g < G and step >= 1:
                            pv(g, step - 1, j // 2)
                        if j % 2 == 1 and g >= 1 and step == 0:
                            pv(g - 1, NT - 1, j // 2)
                        if g == -1 and step == 0:
                            project_v(2 + j)
                    if g == -1 and step == 0:
                        project_v(6)
                        project_v(7)
                    if g == -1 and step == 3:
                        counts()

            pe.wait_ge(s_table, 1)
            more = pe.value_load(steps_i[0:1, 0:1], min_val=MIN_STEPS - 1, max_val=STEPS - 1)
            for q in range(2):
                pe.wait_ge(s_att, 2 * (G - 1) + q + 1)
                for t in range(CT):
                    last = pe.transpose(ps[:, q, t * P:(t + 1) * P], att[:, q * CT + t, P:2 * P], ident[:, :])
                last.then_inc(s_aT, 1)
            for m in range(NT // 2):
                pe.wait_ge(s_aTe, m // 2 + 1)
                for t in (2 * m, 2 * m + 1):
                    last = pe.matmul(ps[:, 2 + m, t % 2 * D:(t % 2 + 1) * D], attT[:, t * P:(t + 1) * P],
                                     w_out_sb[:, 1, :], start=True, stop=True)
                last.then_inc(s_op, 1)

            pe.wait_ge(s_aTe, 2)

            def transpose_rows(n, u, b, turn):
                pe.wait_ge(s_xg[u], 16 * turn + 16)
                wait_turn(pe, s_Te, n - 1)
                for c in range(DC):
                    last = pe.transpose(ps[:, b, c * P:(c + 1) * P], xg[u][:, c * P:(c + 1) * P], ident[:, :])
                last.then_inc(s_T, 1)

            def gate_up(n, u, b, turn):
                pe.wait_ge(s_Te, n + 1)
                pe.wait_ge(s_wt[u], 16 * turn + 16)
                wait_turn(pe, s_h, n - 1)
                for w in range(2):
                    for c in range(DC):
                        last = pe.matmul(ps[0:I, 2 + b, w * P:(w + 1) * P], wgu[u][:, (2 * c + w) * I:(2 * c + w + 1) * I],
                                         xgT[b][:, c * P:(c + 1) * P], start=(c == 0), stop=(c == DC - 1))
                last.then_inc(s_gu, 1)

            def down(n, u, b, turn):
                pe.wait_ge(s_h, n + 1)
                pe.wait_ge(s_wd[u], 16 * turn + 16)
                pe.matmul(ps[:, 4 + b, 0:D], hh[b], wdn[u], start=True, stop=True).then_inc(s_dn, 1)

            def step(s):
                for u in range(FIRST, U + FIRST):
                    n = s * U + u
                    gate_up(n, u % U, u % 2, s + u // U)
                    transpose_rows(n + 2, (u + 2) % U, u % 2, s + (u + 2) // U)
                    down(n - 1, (u - 1) % U, (u - 1) % 2, s + (u - 1) // U)
                    wait_turn(pe, s_y, n - 1)

            transpose_rows(0, 0, 0, 0)
            transpose_rows(1, 1, 1, 0)
            pe.wait_ge(s_res, NT // 2)
            for n in range(FIRST):
                gate_up(n, n, n, 0)
                transpose_rows(n + 2, n + 2, n, 0)
                if n >= 1:
                    down(n - 1, n - 1, n - 1, 0)
            step(0)
            with pe.Fori(1, STEPS) as s:
                with pe.If(s <= more):
                    step(s)
            down(more * U + U + FIRST - 1, FIRST - 1, FIRST - 1, more + 1)

        @block.vector
        def _(dve):
            chained = [0]

            def link(ins):
                chained[0] += 1
                ins.then_inc(s_vchain, 1)
                dve.wait_ge(s_vchain, chained[0])

            def measure(t):
                dve.wait_ge(s_x[t], 16)
                link(dve.bn_stats(stats[:, t, :], x_sb[:, t, :]))
                link(dve.bn_aggr(moments[:, t, :], stats[:, t, :]))
                dve.tensor_scalar(var_eps[:, t:t + 1], moments[:, t, 1:2], EPS, None, ALU.add).then_inc(s_var, 1)

            def normalise(t):
                dve.wait_ge(s_rstd, sum(t >= border for border in LN_BATCHES))
                dve.tensor_scalar(rows[:, t, 0:D], x_sb[:, t, :], moments[:, t, 0:1], rstd[:, t:t + 1],
                                  ALU.subtract, ALU.mult).then_inc(s_xn, 1)

            def rotate(t):
                dve.wait_ge(s_proj, t + 1)
                if t >= 2:
                    dve.wait_ge(s_rot, t - 1)
                heads = 2 * D // DK
                qk = ps[:, 2 + t % 2, :].rearrange("p (h c) -> p h c", c=DK)

                def table(tab):
                    return tab[:, t, :].rearrange("p (a c) -> p a c", a=1).to_broadcast([P, heads, DK])

                dve.tensor_tensor(rope_c[:, t % 2, :].rearrange("p (h c) -> p h c", c=DK), qk, table(cos_sb),
                                  ALU.mult).then_inc(s_rope, 1)
                for odd in range(2):
                    dve.tensor_tensor(rope_s[:, t % 2, :].rearrange("p (h c) -> p h c", c=DK)[:, :, odd::2],
                                      qk[:, :, 1 - odd::2], table(sin_sb)[:, :, odd::2], ALU.mult).then_inc(s_rope, 1)

            def lo_out(t):
                dve.wait_ge(s_hi, t + 1)
                if t >= 2:
                    dve.wait_ge(s_parts[t % 2], 32 * (t // 2))
                dve.tensor_tensor(part_lo[:, t % 2, :], ps[:, 6 + t % 2, :], part_hi[:, t % 2, :].bitcast(F32),
                                  ALU.subtract).then_inc(s_lo, 1)

            for t in range(NT):
                measure(t)
                if t == LN_BATCHES[1] - 1:
                    for first in range(t + 1):
                        normalise(first)
            normalise(LN_BATCHES[1])
            dve.wait_ge(s_rope_tab, 32)
            for t in range(NT):
                rotate(t)
                if t + LN_BATCHES[1] + 1 < NT:
                    normalise(t + LN_BATCHES[1] + 1)
                if t >= 1:
                    lo_out(t - 1)
            lo_out(NT - 1)
            dve.wait_ge(s_const, CONSTS)

            def choose():
                dve.wait_ge(s_vlog, NT)
                for t in range(NT):
                    last = dve.max(top_v[:, t, :], logits[:, t, :])
                link(last)
                for t in range(NT):
                    dve.match_replace(replaced[:, t, :], top_v[:, t, :], logits[:, t, :], TAKEN)
                    last = dve.max_index(top_i[:, t, :], top_v[:, t, :], logits[:, t, :])
                link(last)
                dve.tensor_scalar(chosen[:, :, :], replaced[:, :, :], TAKEN, None, ALU.is_equal).then_inc(s_chosen, 1)
                dve.tensor_tensor(top_d[:, :, :], top_v[:, :, :], top_v[:, :, 0:1].to_broadcast([P, NT, K]),
                                  ALU.subtract).then_inc(s_d, 1)
                dve.tensor_copy(rows[:, :, EXP:EXP + K], top_i[:, :, :])
                link(dve.tensor_copy(rows[:, :, TOK:TOK + 1], tok_i[:, :].rearrange("p (t a) -> p t a", a=1)))

            def count_and_map():
                dve.wait_ge(s_cnt, 1)
                link(dve.tensor_copy(cnt[:, :], ps[:, 3, 0:E]))
                link(dve.tensor_tensor_scan(end_e[:, :], ones[:, 0:E], cnt[:, :], 0.0, ALU.mult, ALU.add))
                link(dve.tensor_tensor(base_e[:, :], end_e[:, :], cnt[:, :], ALU.subtract))
                link(dve.scalar_tensor_tensor(slot_map[:, :, :], ps[:, 4, :].rearrange("p (t e) -> p t e", e=E), 1.0,
                                              base_e[:, :].rearrange("p (a e) -> p a e", a=1)
                                              .to_broadcast([P, NT, E]), ALU.add, ALU.add))
                dve.sem_inc(s_smap, 1)
                link(dve.tensor_tensor(slot_map[:, :, :], slot_map[:, :, :], chosen[:, :, :], ALU.mult))
                for t in range(NT):
                    last = dve.max(slot_f[:, t, :], slot_map[:, t, :])
                link(last)
                dve.tensor_scalar(slot_i[:, :, :], slot_f[:, :, :], -1.0, None, ALU.add).then_inc(s_sloti, 1)

            def weights():
                dve.wait_ge(s_e, 1)
                link(dve.tensor_reduce(top_s[:, :], top_e[:, :, :], AX.X, ALU.add))
                link(dve.reciprocal(top_r[:, :], top_s[:, :]))
                dve.scalar_tensor_tensor(rows[:, :, WGT:WGT + K], top_e[:, :, :], 0.5,
                                         top_r[:, :].rearrange("p (t a) -> p t a", a=1).to_broadcast([P, NT, K]),
                                         ALU.mult, ALU.mult).then_inc(s_route, 1)

            def tile_counts():
                link(dve.tensor_scalar(n_i[:, 0, :], cnt[:, :], float(P - 1), None, ALU.add))
                link(dve.tensor_scalar(n_i[:, 1, :], n_i[:, 0, :], P.bit_length() - 1, None, ALU.arith_shift_right))
                link(dve.tensor_scalar(n_e[:, :], n_i[:, 1, :], 1.0, None, ALU.max))
                link(dve.tensor_tensor_scan(t_end[:, :], ones[:, 0:E], n_e[:, :], 0.0, ALU.mult, ALU.add))

            def tile_ranges():
                dve.tensor_scalar(steps_f[:, :], t_end[:, E - 1:E], float(-FIRST - 1), None, ALU.add)
                link(dve.tensor_tensor(t_beg[:, :], t_end[:, :], n_e[:, :], ALU.subtract))
                dve.tensor_scalar(steps_i[:, :], steps_f[:, :], U.bit_length() - 1, None, ALU.arith_shift_right)
                dve.scalar_tensor_tensor(shift_e[:, :], t_beg[:, :], -float(P), base_e[:, :], ALU.mult, ALU.add)
                dve.tensor_scalar(is_le[:, 0, :], t_beg[:, :], part[:, 0:1], None, ALU.is_le)
                link(dve.tensor_scalar(is_le[:, 1, :], t_end[:, :], part[:, 0:1], None, ALU.is_le))

            def tile_experts():
                dve.tensor_reduce(col[:, 0:1], is_le[:, 1, :], AX.X, ALU.add)
                link(dve.tensor_tensor(hot[:, :], is_le[:, 0, :], is_le[:, 1, :], ALU.subtract))
                dve.tensor_tensor_reduce(junk_e[:, 0, :], hot[:, :], shift_e[:, :], 1.0, 0.0, ALU.mult, ALU.add,
                                         col[:, 1:2])
                link(dve.tensor_tensor_reduce(junk_e[:, 1, :], hot[:, :], end_e[:, :], 1.0, 0.0, ALU.mult, ALU.add,
                                              col[:, 2:3]))

            def tile_columns():
                dve.tensor_scalar(col[:, 3:4], col[:, 0:1], float(E - 1), None, ALU.min)
                link(dve.scalar_tensor_tensor(col[:, 4:5], part[:, 0:1], float(P), col[:, 1:2], ALU.mult, ALU.add))
                link(dve.tensor_scalar(col[:, 4:5], col[:, 4:5], float(PAIRS), None, ALU.min))
                link(dve.tensor_tensor(col[:, 5:6], col[:, 2:3], col[:, 4:5], ALU.subtract))
                for a, c in enumerate((4, 3, 5)):
                    last = dve.tensor_scalar(spread[:, a, :], ident[:, :], col[:, c:c + 1], None, ALU.mult)
                last.then_inc(s_spread, 1)

            def tables():
                link(dve.memset(tile_row[:, 0::2], PAIRS))
                dve.memset(tile_row[:, 1::2], 0)
                dve.memset(tile_e[:, :], 0)
                dve.memset(tile_exp[:, :], 0.0)
                link(dve.tensor_copy(tile_out[:, :], part[:, 1:2].to_broadcast([P, TILES])))
                dve.wait_ge(s_ap, a_no[("table",)] + 1)
                bank = a_bank(("table",))
                dve.tensor_copy(tile_row[0:1, 0:2 * P:2], bank[0:1, 0:P])
                dve.tensor_copy(tile_row[0:1, 1:2 * P:2], bank[0:1, P:2 * P])
                dve.tensor_copy(tile_e[0:1, 0:P], bank[0:1, P:2 * P])
                dve.tensor_copy(tile_exp[:, 0:P], bank[:, P:2 * P])
                dve.tensor_scalar(tile_out[:, 0:P], bank[:, 2 * P:3 * P], part[:, 0:1], part[:, 1:2],
                                  ALU.is_le, ALU.mult).then_inc(s_table, 1)
                dve.wait_ge(s_table, 1)
                dve.sem_inc(s_ad, 1)

            def use_max(g, i, j, u):
                unit = ("max", g, i, j, u)
                lo, width = a_units(i)[u]
                bank = a_bank(unit)[:, 0:width]
                dve.wait_ge(s_ap, a_no[unit] + 1)
                if lo + width == (i + 1) * P:
                    dve.tensor_tensor_reduce(bank, bank, mask_qk[:, HALF - width:HALF], 1.0, TAKEN, ALU.add, ALU.max,
                                             mx[:, g % 2, i // CT, j, i % CT:i % CT + 1]).then_inc(s_ad, 1)
                else:
                    dve.reduce_max(mx_low[:, g % 2, j, i % CT:i % CT + 1], bank, AX.X).then_inc(s_ad, 1)
                if (i, j, u) == (CT, HG - 1, len(a_units(i)) - 1):
                    dve.wait_ge(s_ad, a_no[unit] + 1)
                    dve.tensor_tensor(mx[:, g % 2, 1, :, :], mx[:, g % 2, 1, :, :], mx_low[:, g % 2, :, :],
                                      ALU.max).then_inc(s_mx, 1)

            def use_neg(g, c):
                unit = ("neg", g, c)
                dve.wait_ge(s_ap, a_no[unit] + 1)
                bank = a_bank(unit)[0:HG * CT, 0:P]
                link(dve.tensor_scalar(neg_hi[:, g % 2, c, :], bank, -1.0, None, ALU.mult))
                dve.scalar_tensor_tensor(neg_lo[:, g % 2, c, :], bank, -1.0, neg_hi[:, g % 2, c, :].bitcast(F32),
                                         ALU.mult, ALU.subtract).then_inc(s_neg, 1)
                dve.wait_ge(s_neg, neg_order.index((g, c)) + 1)
                dve.sem_inc(s_ad, 1)

            def use_post(g, q):
                unit = ("post", g, q)
                dve.wait_ge(s_ap, a_no[unit] + 1)
                bank = a_bank(unit).rearrange("p (t h c) -> p t h c", h=HG, c=VW)
                link(dve.reciprocal(rec[:, :, :].rearrange("p t (h a) -> p t h a", a=1), bank[:, :, :, DK:DK + 1]))
                dve.tensor_tensor(
                    att[:, 4 * q:4 * q + 4, g * HG * DK:(g + 1) * HG * DK].rearrange("p t (h c) -> p t h c", c=DK),
                    bank[:, :, :, 0:DK],
                    rec[:, :, :].rearrange("p t (h a) -> p t h a", a=1).to_broadcast([P, 4, HG, DK]),
                    ALU.mult).then_inc(s_att, 1)
                dve.wait_ge(s_att, 2 * g + q + 1)
                dve.sem_inc(s_ad, 1)

            def use_att(t):
                unit = ("att", t)
                if t == 0:
                    dve.wait_ge(s_scat, 16 * NT * K)
                dve.wait_ge(s_ap, a_no[unit] + 1)
                dve.tensor_copy(attT_first[:, t * P:(t + 1) * P], a_bank(unit)[:, 0:P]).then_inc(s_ad, 1)

            def use_out(t):
                unit = ("out", t)
                dve.wait_ge(s_ap, a_no[unit] + 1)
                dve.tensor_tensor(x_sb[:, t, :], a_bank(unit)[:, 0:D], x_sb[:, t, :], ALU.add).then_inc(s_ad, 1)

            tile_steps = {3: tile_counts, 4: tile_ranges, 5: tile_experts, 6: tile_columns}
            use = {"att": use_att, "out": use_out, "table": tables, "max": use_max, "neg": use_neg, "post": use_post}
            for g in range(-1, G + 1):
                for step in range(NT):
                    for j in range(HG):
                        for kind, *what in a_at[(g, step, j)]:
                            use[kind](*what)
                    if g == -1 and step == 1:
                        choose()
                    if g == -1 and step == 4:
                        count_and_map()
                    if g == 0 and step == 1:
                        weights()
                    if g == 1 and step in tile_steps:
                        tile_steps[step]()
            dve.wait_ge(s_table, 1)
            more = dve.value_load(steps_i[0:1, 0:1], min_val=MIN_STEPS - 1, max_val=STEPS - 1)
            dve.wait_ge(s_ad, len(a_order))
            for m in range(NT // 2):
                dve.wait_ge(s_op, m + 1)
                two = x_sb[:, 2 * m:2 * m + 2, :].rearrange("p t d -> p (t d)")
                dve.tensor_tensor(two, ps[:, 2 + m, :], two, ALU.add).then_inc(s_res, 1)


            def meta(n, u, y, turn, added):
                dve.wait_ge(s_xg[u], 16 * turn + 16)
                wait_turn(dve, s_add[y], 16 * added)
                dve.scalar_tensor_tensor(w_junk[y][:, :], xg[u][:, EXP:EXP + K], tile_exp[:, bass.ds(n, 1)],
                                         xg[u][:, WGT:WGT + K], ALU.is_equal, ALU.mult, accum_out=w_slot[y][:, 0:1])
                dve.tensor_tensor(dst[y][:, 0:1], xg[u][:, TOK:TOK + 1], tile_out[:, bass.ds(n, 1)],
                                  ALU.max).then_inc(s_meta, 1)

            def rows_out(n, b):
                dve.wait_ge(s_T, n + 1)
                wait_turn(dve, s_gu, n - 1)
                dve.tensor_copy(xgT[b], ps[:, b, 0:DC * P]).then_inc(s_Te, 1)

            def hidden(n, b):
                dve.wait_ge(s_th, n + 1)
                dve.scalar_tensor_tensor(sg[b], th[b], 1.0, ps[0:I, 2 + b, 0:P],
                                         ALU.add, ALU.mult).then_inc(s_sg, 1)
                dve.wait_ge(s_sg, n + 1)
                wait_turn(dve, s_dn, n - 1)
                dve.tensor_tensor(hh[b], sg[b], ps[0:I, 2 + b, P:2 * P], ALU.mult).then_inc(s_h, 1)

            def step(s):
                for u in range(FIRST, U + FIRST):
                    n = s * U + u
                    rows_out(n + 2, u % 2)
                    hidden(n, u % 2)
                    meta(n, u % U, u % NY, s + u // U, s * (U // NY) + u // NY)

            rows_out(0, 0)
            rows_out(1, 1)
            for n in range(FIRST):
                rows_out(n + 2, n)
                hidden(n, n)
                meta(n, n, n, 0, 0)
            step(0)
            with dve.Fori(1, STEPS) as s:
                with dve.If(s <= more):
                    step(s)

            dve.wait_ge(s_yl[0], 16)
            for k in range(1, NY - 1):
                dve.wait_ge(s_yl[k], 16)
                link(dve.tensor_tensor(sum_buf(0)[:, :, :], sum_buf(0)[:, :, :], sum_buf(k)[:, :, :], ALU.add))
            for q in range(QUARTERS):
                total = sum_buf(0)[:, quarter(q), :]
                dve.wait_ge(s_yq[q], 16)
                dve.tensor_tensor(total, total, sum_buf(NY - 1)[:, quarter(q), :], ALU.add).then_inc(s_fin, 1)


def kernel(**inputs):
    import numpy as np
    import concourse.bacc as bacc
    from concourse.bass_utils import run_bass_kernel_spmd

    f32 = np.float32
    inv = (f32(10000.0) ** (-(np.arange(0, DK, 2, dtype=f32) / f32(DK)))).astype(f32)
    ang = (np.arange(N, dtype=f32)[:, None] * inv).astype(f32)
    cos = np.repeat(np.cos(ang), 2, axis=1).astype(f32)
    sin = np.repeat(np.sin(ang), 2, axis=1).astype(f32) * np.tile(np.array([-1, 1], f32), DK // 2)

    def by_tile(a):
        return np.ascontiguousarray(a.reshape(NT, P, DK).transpose(1, 0, 2))

    a = {k: np.asarray(v) for k, v in inputs.items()}
    w_in = np.concatenate([a["L0_attn_wq"].T, a["L0_attn_wk"].T, a["L0_attn_wv"].T, a["L0_ffn_gate_weight"].T], 1)
    gu = np.concatenate([a["L0_ffn_w_gate"], a["L0_ffn_w_up"]], 2)
    gu = gu.reshape(E, DC, P, 2 * I).transpose(0, 2, 1, 3).reshape(E, P, DC * 2 * I)
    arrays = {
        "x": a["L0_attn_x"].reshape(N, D), "cos": by_tile(cos), "sin": by_tile(sin), "w_in": w_in,
        "w_out": a["L0_attn_wo"].T, "w_gu": gu, "w_down": a["L0_ffn_w_down"],
    }
    arrays = {k: np.ascontiguousarray(v) for k, v in arrays.items()}
    nc = bacc.Bacc("TRN2", target_bir_lowering=False, num_devices=1)
    args = [nc.dram_tensor(k, v.shape, mybir.dt.from_np(v.dtype), kind="ExternalInput").ap() for k, v in arrays.items()]
    out = nc.dram_tensor("out", (N, D), F32, kind="ExternalOutput").ap()
    build(nc, *args, out)
    r = run_bass_kernel_spmd(nc, [arrays], core_ids=[0])
    return r.results[0]["out"].reshape(1, N, D)
```
